# Optimizing a Trainium2 kernel written in Bass

```python
import numpy as np
import jax
import jax.numpy as jnp

def _softmax(x, axis=-1):
    return jax.nn.softmax(x, axis=axis)

def _gelu(x):
    return jax.nn.gelu(x, approximate=True)

def _silu(x):
    return jax.nn.silu(x)

def _sigmoid(x):
    return jax.nn.sigmoid(x)

def _layernorm(x, axis=-1, eps=1e-05):
    m = jnp.mean(x, axis=axis, keepdims=True)
    v = jnp.var(x, axis=axis, keepdims=True)
    return (x - m) / jnp.sqrt(v + eps)

def _scatter_add(tgt, idx, src, axis=0):
    return tgt.at[idx].add(src)

def _segment_sum(src, seg, n):
    return jax.ops.segment_sum(src, seg, n)
kernel_name = 'mk_prb_d1_jaxref_r8_47442a'

def setup_inputs(seed: int=0):
    np.random.seed(seed)
    _w = jnp.asarray

    def _L0_attn_setup():
        import jax, jax.numpy as jnp
        import numpy as np
        B, N, D_MODEL, H = (4, 256, 128, 16)
        key = jax.random.key(seed)
        k1, k2, k3 = jax.random.split(key, 3)
        x = jax.random.normal(k1, (B, N, D_MODEL), dtype=jnp.float32)
        Wqkv = jax.random.normal(k2, (3 * D_MODEL, D_MODEL), dtype=jnp.float32) * 0.02
        bqkv = jnp.zeros((3 * D_MODEL,), dtype=jnp.float32)
        Wo = jax.random.normal(k3, (D_MODEL, D_MODEL), dtype=jnp.float32) * 0.02
        bo = jnp.zeros((D_MODEL,), dtype=jnp.float32)
        return {'x': x, 'Wqkv': Wqkv, 'bqkv': bqkv, 'Wo': Wo, 'bo': bo}
    _L0_attn_in = _L0_attn_setup()

    def _L0_ffn_setup():
        import jax, jax.numpy as jnp
        import numpy as np
        B, S, E, H, NE, TOP_K = (4, 256, 128, 256, 8, 2)
        key = jax.random.key(seed)
        ks = jax.random.split(key, 5)
        s = 0.02
        return {'x': jax.random.normal(ks[0], (B, S, E), jnp.float32), 'w1': jax.random.normal(ks[1], (NE, E, H), jnp.float32) * s, 'b1': jnp.zeros((NE, H), jnp.float32), 'w2': jax.random.normal(ks[2], (NE, H, H), jnp.float32) * s, 'b2': jnp.zeros((NE, H), jnp.float32), 'w3': jax.random.normal(ks[3], (NE, H, E), jnp.float32) * s, 'b3': jnp.zeros((NE, E), jnp.float32), 'gate_w': jax.random.normal(ks[4], (E, NE), jnp.float32) * s, 'gate_b': jnp.zeros((NE,), jnp.float32)}
    _L0_ffn_in = _L0_ffn_setup()
    _d = {'L0_attn_x': _L0_attn_in['x'], 'L0_attn_Wqkv': _L0_attn_in['Wqkv'], 'L0_attn_bqkv': _L0_attn_in['bqkv'], 'L0_attn_Wo': _L0_attn_in['Wo'], 'L0_attn_bo': _L0_attn_in['bo'], 'L0_ffn_w1': _L0_ffn_in['w1'], 'L0_ffn_b1': _L0_ffn_in['b1'], 'L0_ffn_w2': _L0_ffn_in['w2'], 'L0_ffn_b2': _L0_ffn_in['b2'], 'L0_ffn_w3': _L0_ffn_in['w3'], 'L0_ffn_b3': _L0_ffn_in['b3'], 'L0_ffn_gate_w': _L0_ffn_in['gate_w'], 'L0_ffn_gate_b': _L0_ffn_in['gate_b']}
    _x0 = _d['L0_attn_x']
    _d['L0_attn_x'] = jax.random.normal(jax.random.fold_in(jax.random.key(seed), 1), (16, 512, 128), dtype=_x0.dtype)
    del _x0
    return _d

def reference(L0_attn_x, L0_attn_Wqkv, L0_attn_bqkv, L0_attn_Wo, L0_attn_bo, L0_ffn_w1, L0_ffn_b1, L0_ffn_w2, L0_ffn_b2, L0_ffn_w3, L0_ffn_b3, L0_ffn_gate_w, L0_ffn_gate_b):

    def _L0_attn_ref(x, Wqkv, bqkv, Wo, bo):
        import jax, jax.numpy as jnp
        import numpy as np
        B, N, D_MODEL, H = (4, 256, 128, 16)
        b, n, _ = x.shape
        qkv = x @ Wqkv.T + bqkv
        qkv = qkv.reshape(b, n, H, -1).transpose(0, 2, 1, 3)
        q, k, v = jnp.split(qkv, 3, axis=-1)
        scale = k.shape[-1] ** 0.5
        scores = jnp.einsum('bhqd,bhkd->bhqk', q, k) / scale
        attn = jax.nn.softmax(scores, axis=-1)
        out = jnp.einsum('bhqk,bhkd->bhqd', attn, v)
        out = out.transpose(0, 2, 1, 3).reshape(b, n, -1)
        return out @ Wo.T + bo

    def _L0_ffn_ref(x, w1, b1, w2, b2, w3, b3, gate_w, gate_b):
        import jax, jax.numpy as jnp
        import numpy as np
        B, S, E, H, NE, TOP_K = (4, 256, 128, 256, 8, 2)
        gate_weights = jax.nn.softmax(x @ gate_w + gate_b, axis=-1)
        topk_vals, topk_idx = jax.lax.top_k(gate_weights, TOP_K)
        h = jax.nn.gelu(jnp.einsum('bse,neh->bsnh', x, w1) + b1, approximate=False)
        h = jax.nn.gelu(jnp.einsum('bsnh,nhk->bsnk', h, w2) + b2, approximate=False)
        expert_out = jnp.einsum('bsnh,nhe->bsne', h, w3) + b3
        gathered = jnp.take_along_axis(expert_out, topk_idx[..., None], axis=2)
        return jnp.sum(topk_vals[..., None] * gathered, axis=2)
    x = L0_attn_x
    xn = _layernorm(x, axis=-1)
    x = x + _L0_attn_ref(xn, L0_attn_Wqkv, L0_attn_bqkv, L0_attn_Wo, L0_attn_bo) + _L0_ffn_ref(xn, L0_ffn_w1, L0_ffn_b1, L0_ffn_w2, L0_ffn_b2, L0_ffn_w3, L0_ffn_b3, L0_ffn_gate_w, L0_ffn_gate_b)
    return x

_drawn_inputs = setup_inputs


def setup_inputs(seed=0):
    import zlib

    import numpy as np

    out = dict(_drawn_inputs(seed))
    spreads = {'L0_attn_bqkv': (0.0, 0.357),
     'L0_attn_bo': (0.0, 0.1),
     'L0_ffn_b1': (0.0, 0.8),
     'L0_ffn_b2': (0.0, 0.8),
     'L0_ffn_b3': (0.0, 0.334),
     'L0_ffn_gate_b': (0.0, 0.474)}
    factors = {'L0_attn_Wqkv': 8.0,
     'L0_ffn_w1': 8.0,
     'L0_ffn_w2': 8.0,
     'L0_ffn_w3': 8.0,
     'L0_ffn_gate_w': 2.89}
    for name, (base, spread) in spreads.items():
        noise = np.random.default_rng([zlib.crc32(name.encode()), seed]).standard_normal(out[name].shape)
        drawn = base * np.exp(spread * noise) if base else spread * noise
        out[name] = jnp.asarray(drawn.astype(out[name].dtype))
    for name, factor in factors.items():
        out[name] = (out[name] * factor).astype(out[name].dtype)
    return out
```

```python
import concourse.bass as bass
from concourse import mybir
from contextlib import ExitStack

F32, BF16, I32, U32 = mybir.dt.float32, mybir.dt.bfloat16, mybir.dt.int32, mybir.dt.uint32
ALU, ACT, AX = mybir.AluOpType, mybir.ActivationFunctionType, mybir.AxisListType
P = 128
HEADS, HD = 16, 8
NB, SEQ, D = 16, 512, 128
CH = SEQ // P
TILES = NB * CH
NE, HID = 8, 256
SPLITS = 3
STACK = SPLITS * SPLITS * HD
SROWS = STACK + SPLITS
QUAD = 4
UNITS = HEADS // QUAD * CH
VW = 9 * HEADS + 24
SLOT = 256
ETILES = 72
WCOLS = HID + 2 * HID + 2 * D + D + 4
W2AT, W3AT, B3AT, BIAT = HID, 3 * HID, 3 * HID + 2 * D, 3 * HID + 3 * D
MOE0, MOE1, PER = 4, 12, 9
assert (MOE1 - MOE0) * PER == ETILES and ETILES * SLOT >= 2 * NB * SEQ + NE * (SLOT - 1)
EPS = 1e-5
SCALE = 1.0 / float(HD) ** 0.5


def build_block_kernel(nc, x, wq, wk, wv, wo, bq, bk, bv, bo, gate_w, gate_b, wall, ident, tri, iota, prio, out):
    with ExitStack() as ctx:
        def sb(name, shape, dt=F32):
            return ctx.enter_context(nc.sbuf_tensor(name, shape, dt))

        def sem(name):
            return ctx.enter_context(nc.semaphore(name))

        xn = sb("xn", [P, TILES, D])
        wq_s, wk_s, wv_s, wo_s = (sb(n, [P, P]) for n in ("wq_s", "wk_s", "wv_s", "wo_s"))
        bq_s, bk_s = sb("bq_s", [P, 1]), sb("bk_s", [P, 1])
        bv_s, bo_s = sb("bv_s", [P, D]), sb("bo_s", [P, D])
        gw_s, gb_s = sb("gw_s", [P, NE]), sb("gb_s", [P, NE])
        ident_s, ident_b = sb("ident_s", [P, P]), sb("ident_b", [P, P], BF16)
        prio_s, iota_s = sb("prio_s", [P, NE]), sb("iota_s", [P, ETILES])
        stats, small = sb("stats", [P, TILES, 6]), sb("small", [P, 6, TILES])
        gate1, gate2 = sb("gate1", [P, TILES]), sb("gate2", [P, TILES])
        slots = sb("slots", [P, 2, TILES], U32)
        etile = sb("etile", [P, ETILES], U32)
        xq_rows, xv_rows = sb("xq_rows", [P, CH, D]), sb("xv_rows", [P, CH, D])
        xqT, xvT = sb("xqT", [P, SEQ]), sb("xvT", [P, SEQ])
        qk_f, qk_r = sb("qk_f", [P, 2, SEQ]), sb("qk_r", [P, SEQ])
        parts = sb("parts", [P, 2, SPLITS, SEQ], BF16)
        qstack = [sb(f"qstack{i}", [P, HEADS, SEQ], BF16) for i in range(2)]
        kstack = [sb(f"kstack{i}", [P, HEADS, SEQ], BF16) for i in range(2)]
        v_s = [sb(f"v_s{i}", [P, CH, VW]) for i in range(2)]
        probs = sb("probs", [P, CH, QUAD, SEQ])
        mx, mr = sb("mx", [P, CH, HEADS]), sb("mr", [P, CH, HEADS])
        mparts = sb("mparts", [P, CH, SPLITS * HEADS], BF16)
        mT = sb("mT", [SPLITS * HEADS, SEQ], BF16)
        ot = sb("ot", [P, HEADS // QUAD, SEQ])
        rden, att = sb("rden", [P, CH, HEADS]), sb("att", [P, CH, D])
        attT, xres = sb("attT", [P, SEQ]), sb("xres", [P, CH, D])
        w_e = [sb(f"w_e{i}", [P, WCOLS]) for i in range(3)]
        xs = [sb(f"xs{i}", [P, 2, D]) for i in range(3)]
        ys = [sb(f"ys{i}", [P, 2, D]) for i in range(3)]
        xT = [sb(f"xT{i}", [P, SLOT]) for i in range(2)]
        h1, h2 = sb("h1", [P, 2, SLOT]), sb("h2", [P, 2, SLOT])
        ring = probs[:, :, :, :].rearrange("p a b c -> p (a b c)")

        def work(n):
            return ring[:, n * 512:(n + 1) * 512]

        tri_f, tri_b, ones_b = work(13)[:, 0:P], work(12)[:, 0:64].bitcast(BF16), work(12)[:, 64:128].bitcast(BF16)
        gate_xT = [work(14), work(15)]
        pair_b = work(11)[:, 0:256].bitcast(BF16)
        gathered = [w_e[i][:, 0:2 * CH * D].rearrange("p (k d) -> p k d", d=D) for i in range(2)]
        outbuf = [w_e[2][:, i * CH * D:(i + 1) * CH * D].rearrange("p (c d) -> p c d", d=D) for i in range(2)]
        zeros = w_e[2][:, 0:8 * D]

        psS = ctx.enter_context(nc.psum_tensor("psS", [P, 4, 512], F32))
        psM = ctx.enter_context(nc.psum_tensor("psM", [P, 2, 512], F32))
        psV = ctx.enter_context(nc.psum_tensor("psV", [P, 512], F32))
        psX = ctx.enter_context(nc.psum_tensor("psX", [P, 512], F32))
        psMT = psV[:, 0:256].bitcast(BF16)

        stack_d = nc.dram_tensor("stack_rows", [2, 2, STACK, HEADS, SEQ], BF16, kind="Internal").ap()
        max_d = nc.dram_tensor("max_rows", [2, SPLITS * HEADS, SEQ], BF16, kind="Internal").ap()
        xs_d = nc.dram_tensor("slot_rows", [ETILES * SLOT, D], F32, kind="Internal").ap()
        ys_d = nc.dram_tensor("slot_outs", [ETILES * SLOT, D], F32, kind="Internal").ap()
        xs_v = xs_d.rearrange("(n p c) d -> n p (c d)", p=P, c=2)
        ys_v = ys_d.rearrange("(n p c) d -> n p (c d)", p=P, c=2)
        x_v = x.rearrange("b (p c) d -> b p (c d)", c=CH)
        out_v = out.rearrange("b (p c) d -> b p (c d)", c=CH)

        s_const, s_zero, s_cst, s_zset = sem("s_const"), sem("s_zero"), sem("s_cst"), sem("s_zset")
        s_ones = sem("s_ones")
        CONSTANTS = 16 * 14
        s_x = [sem(f"s_x{i}") for i in range(2)]
        s_dve = sem("s_dve")
        s_var, s_sd = sem("s_var"), sem("s_sd")
        s_xn = [sem(f"s_xn{i}") for i in range(2)]
        s_gxt, s_gx, s_logit = sem("s_gxt"), sem("s_gx"), sem("s_logit")
        s_lread = sem("s_lread")
        s_gshift, s_gexp = sem("s_gshift"), sem("s_gexp")
        s_pick, s_rank, s_ranked, s_slots = sem("s_pick"), sem("s_rank"), sem("s_ranked"), sem("s_slots")
        s_xqrow, s_xqt, s_xq = sem("s_xqrow"), sem("s_xqt"), sem("s_xq")
        s_xvrow, s_xvt, s_xv = sem("s_xvrow"), sem("s_xvt"), sem("s_xv")
        s_qp, s_kp, s_qf, s_kf = sem("s_qp"), sem("s_kp"), sem("s_qf"), sem("s_kf")
        s_part, s_rows = sem("s_part"), sem("s_rows")
        s_stack = [[sem(f"s_stack{i}{q}") for q in range(HEADS // QUAD)] for i in range(2)]
        s_vp, s_v = sem("s_vp"), sem("s_v")
        s_mxmm, s_mx, s_mp = sem("s_mxmm"), sem("s_mx"), sem("s_mp")
        s_mt, s_mT, s_mw, s_mrow = sem("s_mt"), sem("s_mT"), sem("s_mw"), sem("s_mrow")
        s_st, s_exp, s_pvu, s_ot = sem("s_st"), sem("s_exp"), sem("s_pvu"), sem("s_ot")
        s_outt, s_rd, s_norm = sem("s_outt"), sem("s_rd"), sem("s_norm")
        s_att, s_attT, s_wo = sem("s_att"), sem("s_attT"), sem("s_wo")
        s_xres, s_xb, s_res = sem("s_xres"), sem("s_xb"), sem("s_res")
        s_scat = sem("s_scat")
        s_w = [sem(f"s_w{i}") for i in range(3)]
        s_xs = [sem(f"s_xs{i}") for i in range(3)]
        s_yst = [sem(f"s_yst{i}") for i in range(3)]
        s_xt, s_xT, s_h1m, s_h1 = sem("s_xt"), sem("s_xT"), sem("s_h1m"), sem("s_h1")
        s_h2m, s_h2, s_ym, s_y = sem("s_h2m"), sem("s_h2"), sem("s_ym"), sem("s_y")
        s_gath = [sem(f"s_gath{i}") for i in range(2)]
        s_out = [sem(f"s_out{i}") for i in range(2)]
        AHEAD = 1
        s_half, s_comb = sem("s_half"), sem("s_comb")
        s_settled = sem("s_settled")

        AUX = ["pv_last", "xq_turn", "xv_turn", "max_turn", "q_proj", "v_proj", "k_proj",
               "out0", "out1", "out2", "out3", "att_turn", "wo"]

        def between(b, moe):
            aux = [(a, None) for a in AUX]
            if isinstance(b, int) and b + 3 >= NB:
                aux = [a for a in aux if a[0] not in ("xq_turn", "q_proj", "k_proj")]
            if isinstance(b, int) and b + 1 >= NB:
                aux = [a for a in aux if a[0] not in ("xv_turn", "max_turn", "v_proj")]
            if not moe:
                return aux
            steps = [aux.pop(0), ("slot_turn", 0), aux.pop(0), ("slot_turn", 1), ("up", 0), aux.pop(0), aux.pop(0)]
            for t in range(PER):
                steps.append(("mid", t))
                if t + 1 < PER:
                    steps.append(("up", t + 1))
                if t + 2 < PER:
                    steps.append(("slot_turn", t + 2))
                steps += [aux.pop(0)] if aux else []
                steps.append(("down", t))
            return steps + aux

        def settle(eng):
            eng.sem_inc(s_settled, 1)

        def has_qk(b):
            return not isinstance(b, int) or b + 3 < NB

        def has_next(b):
            return not isinstance(b, int) or b + 1 < NB

        COMBINED = {12: range(0, 5), 13: range(5, 10), 14: range(10, 14), 15: range(14, 15)}

        def combined(b):
            return COMBINED.get(b, range(0)) if isinstance(b, int) else range(0)

        def batches(eng, body, loop_first=True):
            if loop_first:
                with eng.Fori(0, MOE0 // 2) as i:
                    for par in range(2):
                        body(2 * i + par, i, par, False)
            else:
                for b in range(MOE0):
                    body(b, b // 2, b % 2, False)
            with eng.Fori(MOE0 // 2, MOE1 // 2) as i:
                for par in range(2):
                    body(2 * i + par, i, par, True)
            for b in range(MOE1, NB):
                body(b, b // 2, b % 2, False)

        block = ctx.enter_context(nc.Block())

        @block.sync
        def _(sp):
            for dst, src in ((xn[:, 0:2 * CH, :].rearrange("p (b c) d -> p b (c d)", c=CH), x_v[0:2]),
                             (xn[:, 2 * CH:4 * CH, :].rearrange("p (b c) d -> p b (c d)", c=CH), x_v[2:4])):
                sp.dma_start(dst, src.rearrange("b p k -> p b k")).then_inc(s_x[0], 16)
            for dst, src in ((ident_s[:, :], ident), (wq_s[:, :], wq), (wk_s[:, :], wk), (wv_s[:, :], wv),
                             (wo_s[:, :], wo), (bq_s[:, :], bq), (bk_s[:, :], bk),
                             (bv_s[:, :], bv.partition_broadcast(P)), (bo_s[:, :], bo.partition_broadcast(P)),
                             (gw_s[:, :], gate_w), (gb_s[:, :], gate_b.partition_broadcast(P)),
                             (prio_s[:, :], prio.partition_broadcast(P)), (iota_s[:, :], iota.partition_broadcast(P)),
                             (tri_f, tri)):
                sp.dma_start(dst, src).then_inc(s_const, 16)
            for b in range(4, NB, 2):
                sp.dma_start(xn[:, CH * b:CH * (b + 2), :].rearrange("p (b c) d -> p b (c d)", c=CH),
                             x_v[b:b + 2].rearrange("b p k -> p b k")).then_inc(s_x[1], 16)

            def write_rows(g, pair, par):
                sp.wait_ge(s_part, 8 * (g + 1))
                settle(sp)
                if not isinstance(g, int) or g >= 2:
                    for q in range(HEADS // QUAD):
                        sp.wait_ge(s_stack[par][q], 32 * pair)
                for i in range(SPLITS):
                    for j in range(SPLITS):
                        s = SPLITS * i + j
                        for side, part in ((0, i), (1, j)):
                            sp.dma_start(stack_d[side, par, HD * s:HD * (s + 1)].rearrange("d h t -> h d t"),
                                         parts[:, side, part, :]).then_inc(s_rows, 16)

            def read_rows(par, q):
                for side, stack in ((0, qstack), (1, kstack)):
                    sp.dma_start(stack[par][0:STACK, QUAD * q:QUAD * (q + 1), :],
                                 stack_d[side, par, :, QUAD * q:QUAD * (q + 1), :]).then_inc(s_stack[par][q], 16)

            def write_max(g, par):
                sp.wait_ge(s_mT, g + 1)
                sp.dma_start(max_d[par], mT[:, :]).then_inc(s_mw, 16)
                sp.wait_ge(s_mw, 16 * (g + 1))
                sp.dma_start(qstack[par][STACK:SROWS, :, :],
                             max_d[par].rearrange("(s h) t -> s h t", s=SPLITS)).then_inc(s_mrow, 16)

            def load_tile(n, t, first):
                if not first:
                    sp.wait_ge(s_y, AHEAD + n - 2)
                settle(sp)
                e = sp.value_load(etile[0:1, bass.ds(n, 1)], min_val=0, max_val=NE - 1)
                sp.dma_start(w_e[t % 3][:, :], wall[bass.ds(e, 1)].rearrange("e p n -> (e p) n")) \
                    .then_inc(s_w[t % 3], 16)
                sp.dma_start(xs[t % 3][:, :, :].rearrange("p c d -> p (c d)"),
                             xs_v[bass.ds(n, 1)].rearrange("n p k -> (n p) k")).then_inc(s_xs[t % 3], 16)

            for g in range(3):
                if g:
                    sp.wait_ge(s_xqt, g)
                else:
                    sp.wait_ge(s_xn[0], 1)
                sp.dma_start(xq_rows[:, :, :], xn[:, CH * g:CH * (g + 1), :]).then_inc(s_xqrow, 16)
                if g == 0:
                    sp.dma_start(xv_rows[:, :, :], xn[:, 0:CH, :]).then_inc(s_xvrow, 16)
                write_rows(g, g // 2, g % 2)
                if g < 2:
                    sp.wait_ge(s_rows, 18 * 16 * (g + 1))
                    sp.wait_ge(s_ones, 4)
                    for q in range(HEADS // QUAD):
                        read_rows(g, q)
                if g == 0:
                    sp.wait_ge(s_zset, 1)
                    for r in range(0, ETILES * SLOT, 8 * P):
                        sp.dma_start(xs_d[r:r + 8 * P, :].rearrange("(p r) d -> p (r d)", p=P),
                                     zeros).then_inc(s_zero, 16)
            write_max(0, 0)

            def body(b, i, par, moe):
                late = list(combined(b))
                if has_qk(b):
                    if not moe:
                        sp.wait_ge(s_xn[1], 1)
                    sp.wait_ge(s_xqt, b + 3)
                    sp.dma_start(xq_rows[:, :, :], xn[:, bass.ds(CH * (b + 3), CH), :]).then_inc(s_xqrow, 16)
                if has_next(b):
                    sp.wait_ge(s_xvt, b + 1)
                    sp.dma_start(xv_rows[:, :, :], xn[:, bass.ds(CH * (b + 1), CH), :]).then_inc(s_xvrow, 16)
                sp.wait_ge(s_res, AHEAD + b)
                sp.dma_start(xres[:, :, :].rearrange("p c d -> p (c d)"),
                             x_v[bass.ds(b, 1)].rearrange("b p k -> (b p) k")).then_inc(s_xres, 16)
                if not isinstance(b, int) or b + 2 < NB:
                    sp.wait_ge(s_rows, 18 * 16 * (b + 3))
                    for q in range(HEADS // QUAD):
                        sp.wait_ge(s_st, 2 * UNITS * b + 2 * CH * (q + 1))
                        read_rows(par, q)
                        if late:
                            store_out(late.pop(0))
                for g in late:
                    store_out(g)
                if moe:
                    sp.wait_ge(s_scat, 2 * 16 * TILES)
                    for t in range(3):
                        n = PER * (b - MOE0) + t
                        sp.wait_ge(s_y, AHEAD + PER * (b - MOE0))
                        load_tile(n, t, True)
                if has_next(b):
                    write_max(b + 1, 1 - par)
                for t in range(PER if moe else 0):
                    n = PER * (b - MOE0) + t
                    sp.wait_ge(s_y, AHEAD + n + 1)
                    sp.dma_start(ys_v[bass.ds(n, 1)].rearrange("n p k -> (n p) k"),
                                 ys[t % 3][:, :, :].rearrange("p c d -> p (c d)")).then_inc(s_yst[t % 3], 16)
                    if t + 3 < PER:
                        load_tile(n + 3, t, False)
                if has_qk(b):
                    write_rows(b + 3, i + (par + 3) // 2, 1 - par)

            def store_out(g):
                sp.wait_ge(s_comb, g + 1)
                sp.dma_start(out_v[g], outbuf[g % 2].rearrange("p c d -> p (c d)")).then_inc(s_out[g % 2], 16)

            batches(sp, body)
            store_out(NB - 1)
            for i in range(2):
                sp.wait_ge(s_out[i], 16 * NB // 2)

        @block.gpsimd
        def _(pool):
            def split(g):
                if not isinstance(g, int) or g >= 1:
                    pool.wait_ge(s_rows, 18 * 16 * g)
                for side, s_f in ((0, s_qf), (1, s_kf)):
                    pool.wait_ge(s_f, g + 1)
                    settle(pool)
                    f, part = qk_f[:, side, :], [parts[:, side, i, :] for i in range(SPLITS)]
                    at = 8 * g + 4 * side
                    pool.tensor_scalar(part[0], f, 1.0, 0.0, ALU.mult, ALU.add).then_inc(s_part, 1)
                    pool.wait_ge(s_part, at + 1)
                    pool.tensor_tensor(qk_r[:, :], f, part[0], ALU.subtract).then_inc(s_part, 1)
                    pool.wait_ge(s_part, at + 2)
                    settle(pool)
                    pool.tensor_scalar(part[1], qk_r[:, :], 1.0, 0.0, ALU.mult, ALU.add).then_inc(s_part, 1)
                    pool.wait_ge(s_part, at + 3)
                    pool.tensor_tensor(part[2], qk_r[:, :], part[1], ALU.subtract).then_inc(s_part, 1)
                    pool.wait_ge(s_part, at + 4)

            def scatter(g):
                for t in range(CH * g, CH * (g + 1)):
                    for k in range(2):
                        pool.indirect_dma_start(
                            out=xs_d, out_offset=bass.IndirectOffsetOnAxis(ap=slots[:, k, t:t + 1], axis=0),
                            in_=xn[:, t, :], in_offset=None).then_inc(s_scat, 16)

            def gather(g):
                if g >= 2:
                    pool.wait_ge(s_comb, g - 1)
                for k in range(2):
                    for c in range(CH):
                        t = CH * g + c
                        pool.indirect_dma_start(
                            out=gathered[g % 2][:, CH * k + c, :], out_offset=None, in_=ys_d,
                            in_offset=bass.IndirectOffsetOnAxis(ap=slots[:, k, t:t + 1], axis=0)) \
                            .then_inc(s_gath[g % 2], 16)

            for g in range(3):
                split(g)

            def body(b, i, par, moe):
                if isinstance(b, int) and b < MOE0:
                    if b == 0:
                        pool.wait_ge(s_slots, 1)
                        pool.wait_ge(s_zero, 16 * ETILES * SLOT // (8 * P))
                        pool.wait_ge(s_xn[1], 1)
                    else:
                        pool.wait_ge(s_res, AHEAD + b)
                    for g in range(4 * b, 4 * b + 4):
                        scatter(g)
                for g in combined(b):
                    if g == 0:
                        for i in range(3):
                            pool.wait_ge(s_yst[i], 16 * AHEAD + 16 * ETILES // 3)
                    gather(g)
                pool.wait_ge(s_xres, 16 * (b + 1))
                pool.tensor_tensor(xres[:, :, :], xres[:, :, :], bo_s[:, None, :].to_broadcast([P, CH, D]),
                                   ALU.add).then_inc(s_xb, 1)
                if has_qk(b):
                    split(b + 3)

            pool.wait_ge(s_const, CONSTANTS)
            batches(pool, body, loop_first=False)
            gather(NB - 1)

        @block.scalar
        def _(act):
            def deviation(i):
                act.wait_ge(s_var, i + 1)
                t0, t1 = ((0, 16), (16, TILES))[i]
                act.activation(small[:, 3, t0:t1], small[:, 2, t0:t1], ACT.Sqrt).then_inc(s_sd, 1)

            def step(kind, t, b):
                if kind == "pv_last":
                    act.wait_ge(s_pvu, UNITS * (b + 1))
                    act.activation(ot[:, 3, :], psV[:, :], ACT.Copy).then_inc(s_ot, 1)
                elif kind == "xq_turn":
                    act.wait_ge(s_xqt, b + 4)
                    act.activation(xqT[:, :], psX[:, :], ACT.Copy).then_inc(s_xq, 1)
                elif kind == "q_proj":
                    act.wait_ge(s_qp, b + 4)
                    if not isinstance(b, int) or b > -3:
                        act.wait_ge(s_part, 8 * (b + 3))
                    act.activation(qk_f[:, 0, :], psM[:, 1, :], ACT.Identity, bias=bq_s[:, 0:1]).then_inc(s_qf, 1)
                elif kind == "k_proj":
                    act.wait_ge(s_kp, b + 4)
                    act.activation(qk_f[:, 1, :], psX[:, :], ACT.Identity, bias=bk_s[:, 0:1]).then_inc(s_kf, 1)
                elif kind == "att_turn":
                    act.wait_ge(s_att, b + 1)
                    act.activation(attT[:, :], psM[:, 1, :], ACT.Copy).then_inc(s_attT, 1)
                elif kind in ("up", "mid"):
                    n = PER * (b - MOE0) + t
                    mm, done, bank, dst, at = (s_h1m, s_h1, 0, h1, BIAT) if kind == "up" else \
                        (s_h2m, s_h2, 1, h2, BIAT + 2)
                    act.wait_ge(mm, n + 1)
                    for c in range(2):
                        act.activation(dst[:, c, :], psS[:, bank, c * SLOT:(c + 1) * SLOT], ACT.Gelu,
                                       bias=w_e[t % 3][:, at + c:at + c + 1]).then_inc(done, 1)

            act.wait_ge(s_const, CONSTANTS)
            deviation(0)
            for b in (-3, -2):
                for kind in ("xq_turn", "q_proj", "k_proj"):
                    step(kind, None, b)
            deviation(1)
            for g in range(NB):
                act.wait_ge(s_gxt, g + 1)
                if g >= 2:
                    act.wait_ge(s_logit, g - 1)
                act.activation(gate_xT[g % 2], psS[:, g % 4, :], ACT.Copy).then_inc(s_gx, 1)
            for kind in ("xq_turn", "q_proj", "k_proj"):
                step(kind, None, -1)
            act.wait_ge(s_gshift, 1)
            act.activation(work(2), work(1), ACT.Exp).then_inc(s_gexp, 1)
            act.wait_ge(s_slots, 1)

            def body(b, i, par, moe):
                for u in range(UNITS):
                    for half in range(2):
                        act.wait_ge(s_st, 2 * UNITS * b + 2 * u + half + 1)
                        if u >= CH and half == 0:
                            act.wait_ge(s_pvu, UNITS * b + u - CH + 1)
                        act.activation(probs[:, u % CH, 2 * half:2 * half + 2, :],
                                       psS[:, 2 * half:2 * half + 2, :], ACT.Exp, scale=SCALE).then_inc(s_exp, 1)
                    if u % CH == 0 and u:
                        q = u // CH - 1
                        act.wait_ge(s_pvu, UNITS * b + CH * (q + 1))
                        act.activation(ot[:, q, :], psV[:, :], ACT.Copy).then_inc(s_ot, 1)
                for kind, t in between(b, moe):
                    step(kind, t, b)

            batches(act, body)

        @block.tensor
        def _(pe):
            def turn_rows(dst, rows, done):
                for c in range(CH):
                    mm = pe.transpose(dst[:, c * P:(c + 1) * P], rows[:, c, :], ident_s[:, :])
                mm.then_inc(done, 1)

            def max_unit(g, pair, par, h, chunks):
                if h % QUAD == 0 and chunks[0] == 0:
                    pe.wait_ge(s_stack[par][h // QUAD], 32 * (pair + 1))
                for c in chunks:
                    i = CH * h + c
                    if i >= 2:
                        pe.wait_ge(s_mx, 4 * HEADS * g + i - 1)
                    pe.matmul(psM[:, i % 2, :], qstack[par][0:STACK, h, c * P:(c + 1) * P],
                              kstack[par][0:STACK, h, :], start=True, stop=True).then_inc(s_mxmm, 1)

            def pv_unit(b, par, u):
                q, kc = u // CH, u % CH
                pe.wait_ge(s_exp, 2 * UNITS * b + 2 * u + 2)
                if kc == 0 and q:
                    pe.wait_ge(s_ot, 4 * b + q)
                if u == 0:
                    pe.wait_ge(s_v, b + 1)
                for j in range(QUAD):
                    h = QUAD * q + j
                    mm = pe.matmul(psV[32 * j:32 * (j + 1), :], v_s[par][:, kc, 9 * h:9 * h + 32],
                                   probs[:, u % CH, j, :], start=(kc == 0), stop=(kc == CH - 1),
                                   tile_position=(0, 32 * j))
                mm.then_inc(s_pvu, 1)
                return mm

            def step(kind, t, b, par):
                if kind == "pv_last":
                    pv_unit(b, par, UNITS - 1)
                elif kind == "xq_turn":
                    pe.wait_ge(s_xqrow, 16 * (b + 4))
                    turn_rows(psX, xq_rows, s_xqt)
                elif kind == "xv_turn":
                    pe.wait_ge(s_xvrow, 16 * (b + 2))
                    if not (isinstance(b, int) and b < 0):
                        pe.wait_ge(s_mx, 4 * HEADS * (b + 2))
                    turn_rows(psM[:, 0, :], xv_rows, s_xvt)
                elif kind == "max_turn":
                    pe.wait_ge(s_mp, 4 * (b + 2))
                    if not (isinstance(b, int) and b < 0):
                        pe.wait_ge(s_ot, 4 * b + 4)
                    settle(pe)
                    for c in range(CH):
                        mm = pe.transpose(psMT[0:SPLITS * HEADS, c * P:(c + 1) * P], mparts[:, c, :], ident_b[:, :])
                    mm.then_inc(s_mt, 1)
                elif kind == "q_proj":
                    pe.wait_ge(s_xq, b + 4)
                    pe.matmul(psM[:, 1, :], wq_s[:, :], xqT[:, :], start=True, stop=True).then_inc(s_qp, 1)
                elif kind == "k_proj":
                    pe.matmul(psX[:, :], wk_s[:, :], xqT[:, :], start=True, stop=True).then_inc(s_kp, 1)
                elif kind == "v_proj":
                    pe.wait_ge(s_xv, b + 2)
                    for c in range(CH):
                        mm = pe.matmul(psM[:, 0, c * P:(c + 1) * P], xvT[:, c * P:(c + 1) * P], wv_s[:, :],
                                       start=True, stop=True)
                    mm.then_inc(s_vp, 1)
                elif kind in ("out0", "out1", "out2", "out3"):
                    c = int(kind[3])
                    if c == 0:
                        pe.wait_ge(s_ot, 4 * b + 4)
                        if has_next(b):
                            pe.wait_ge(s_mT, b + 2)
                    elif c == 1 and has_qk(b):
                        pe.wait_ge(s_qf, b + 4)
                    elif c == 1 and has_next(b):
                        pe.wait_ge(s_mx, 4 * HEADS * (b + 2))
                    elif c == 2 and has_next(b):
                        pe.wait_ge(s_v, b + 2)
                    elif c == 2:
                        pe.wait_ge(s_res, AHEAD + b)
                    elif c == 3 and has_qk(b):
                        pe.wait_ge(s_kf, b + 4)
                    dst = (psV[:, :], psM[:, 1, :], psM[:, 0, :], psX[:, :])[c]
                    for q in range(HEADS // QUAD):
                        mm = pe.transpose(dst[:, q * P:(q + 1) * P], ot[:, q, c * P:(c + 1) * P], ident_s[:, :])
                    mm.then_inc(s_outt, 1)
                elif kind == "att_turn":
                    pe.wait_ge(s_norm, CH * (b + 1))
                    turn_rows(psM[:, 1, :], att, s_att)
                elif kind == "wo":
                    pe.wait_ge(s_attT, b + 1)
                    for c in range(CH):
                        mm = pe.matmul(psM[:, 0, c * P:(c + 1) * P], attT[:, c * P:(c + 1) * P], wo_s[:, :],
                                       start=True, stop=True)
                    mm.then_inc(s_wo, 1)
                else:
                    n, w = PER * (b - MOE0) + t, w_e[t % 3]
                    third = 16 * (PER // 3 * (b - MOE0) + t // 3 + 1)
                    if kind == "slot_turn":
                        pe.wait_ge(s_xs[t % 3], third)
                        if t:
                            pe.wait_ge(s_xT, n)
                        for c in range(2):
                            mm = pe.transpose(psS[:, 2, c * P:(c + 1) * P], xs[t % 3][:, c, :], ident_s[:, :])
                        mm.then_inc(s_xt, 1)
                    elif kind == "up":
                        pe.wait_ge(s_w[t % 3], third)
                        pe.wait_ge(s_xT, n + 1)
                        if t:
                            pe.wait_ge(s_h1, 2 * n)
                        for c in range(2):
                            mm = pe.matmul(psS[:, 0, c * SLOT:(c + 1) * SLOT], w[:, c * P:(c + 1) * P],
                                           xT[t % 2][:, :], start=True, stop=True)
                        mm.then_inc(s_h1m, 1)
                    elif kind == "mid":
                        pe.wait_ge(s_h1, 2 * n + 2)
                        if t:
                            pe.wait_ge(s_h2, 2 * n)
                        for c in range(2):
                            for k in range(2):
                                at = W2AT + k * HID + c * P
                                mm = pe.matmul(psS[:, 1, c * SLOT:(c + 1) * SLOT], w[:, at:at + P], h1[:, k, :],
                                               start=(k == 0), stop=(k == 1))
                        mm.then_inc(s_h2m, 1)
                    elif kind == "down":
                        pe.wait_ge(s_h2, 2 * n + 2)
                        if t:
                            pe.wait_ge(s_y, AHEAD + n)
                        for c in range(2):
                            for k in range(2):
                                at = W3AT + k * D
                                mm = pe.matmul(psS[:, 3, c * P:(c + 1) * P], h2[:, k, c * P:(c + 1) * P],
                                               w[:, at:at + D], start=(k == 0), stop=(k == 1))
                        mm.then_inc(s_ym, 1)

            pe.wait_ge(s_const, CONSTANTS)
            pe.wait_ge(s_cst, 1)
            for kind in ("xq_turn", "q_proj"):
                step(kind, None, -3, 1)
            step("xv_turn", None, -1, 1)
            step("k_proj", None, -3, 1)
            step("v_proj", None, -1, 1)
            pe.wait_ge(s_kf, 1)
            step("xq_turn", None, -2, 0)
            step("q_proj", None, -2, 0)
            step("k_proj", None, -2, 0)
            pe.wait_ge(s_xn[0], 1)
            for g in range(NB + 1):
                if g < NB:
                    if g == 4:
                        pe.wait_ge(s_xn[1], 1)
                    if g >= 4:
                        pe.wait_ge(s_gx, g - 3)
                    turn_rows(psS[:, g % 4, :], xn[:, CH * g:CH * (g + 1), :], s_gxt)
                if g:
                    pe.wait_ge(s_gx, g)
                    for c in range(CH):
                        at = NE * (CH * (g - 1) + c)
                        mm = pe.matmul(psV[:, at:at + NE], gate_xT[(g - 1) % 2][:, c * P:(c + 1) * P], gw_s[:, :],
                                       start=True, stop=True)
                    mm.then_inc(s_logit, 1)
            pe.wait_ge(s_kf, 2)
            step("xq_turn", None, -1, 1)
            pe.wait_ge(s_qf, 2)
            step("q_proj", None, -1, 1)
            step("k_proj", None, -1, 1)
            pe.wait_ge(s_v, 1)
            pe.wait_ge(s_qf, 3)
            for h in range(HEADS):
                max_unit(0, 0, 0, h, range(CH))
            pe.wait_ge(s_lread, 1)
            step("max_turn", None, -1, 1)
            pe.wait_ge(s_pick, 1)
            for i, m in enumerate((tri_b, ones_b)):
                mm = pe.matmul(psM[:, i, :], m, pair_b, start=True, stop=True)
            mm.then_inc(s_rank, 1)
            pe.wait_ge(s_ranked, 1)
            pe.wait_ge(s_mT, 1)

            def body(b, i, par, moe):
                if moe:
                    pe.wait_ge(s_y, AHEAD + PER * (b - MOE0))
                elif isinstance(b, int):
                    pe.wait_ge(s_y, AHEAD + ETILES)
                pe.wait_ge(s_res, AHEAD + b)
                pe.wait_ge(s_mrow, 16 * (b + 1))
                for u in range(UNITS):
                    q, kc = u // CH, u % CH
                    for half in range(2):
                        if u:
                            pe.wait_ge(s_exp, 2 * UNITS * b + 2 * u + half - 1)
                        for j in range(2 * half, 2 * half + 2):
                            h = QUAD * q + j
                            mm = pe.matmul(psS[:, j, :], kstack[par][0:SROWS, h, kc * P:(kc + 1) * P],
                                           qstack[par][0:SROWS, h, :], start=True, stop=True)
                        mm.then_inc(s_st, 1)
                    if has_next(b):
                        max_unit(b + 1, i + (par + 1) // 2, 1 - par, u, range(0, 2))
                    if u:
                        mm = pv_unit(b, par, u - 1)
                    if has_next(b):
                        max_unit(b + 1, i + (par + 1) // 2, 1 - par, u, range(2, CH))
                for kind, t in between(b, moe):
                    step(kind, t, b, par)

            batches(pe, body)

        @block.vector
        def _(dve):
            done = [0]

            def link(ins):
                done[0] += 1
                ins.then_inc(s_dve, 1)
                dve.wait_ge(s_dve, done[0])

            dve.memset(zeros, 0.0).then_inc(s_zset, 1)
            dve.sem_inc(s_res, AHEAD)
            dve.sem_inc(s_y, AHEAD)
            for place in s_yst:
                dve.sem_inc(place, 16 * AHEAD)
            for i in range(2):
                dve.memset(kstack[i][64:96, :, :], 1.0).then_inc(s_ones, 1)
                dve.memset(v_s[i][:, :, :], 1.0).then_inc(s_ones, 1)
            dve.wait_ge(s_const, CONSTANTS)
            dve.tensor_copy(ident_b[:, :], ident_s[:, :])
            dve.tensor_copy(tri_b, tri_f)
            dve.memset(ones_b, 1.0).then_inc(s_cst, 1)

            def layer_norm(i):
                t0, t1 = ((0, 16), (16, TILES))[i]
                dve.wait_ge(s_x[i], 16 * (2, 6)[i])
                for t in range(t0, t1):
                    ins = dve.bn_stats(stats[:, t, :], xn[:, t, :])
                link(ins)
                st = stats[:, t0:t1, :]
                mean, tmp, var, sd, rstd, sq = (small[:, k, t0:t1] for k in range(6))
                dve.tensor_tensor(sq, st[:, :, 1], st[:, :, 4], ALU.subtract)
                dve.tensor_tensor(tmp, st[:, :, 2], st[:, :, 5], ALU.add)
                link(dve.tensor_tensor(mean, st[:, :, 1], st[:, :, 4], ALU.add))
                dve.tensor_scalar(mean, mean, 0.5, None, ALU.mult)
                link(dve.tensor_tensor(sq, sq, sq, ALU.mult))
                link(dve.tensor_scalar(sq, sq, 0.25, EPS, ALU.mult, ALU.add))
                dve.scalar_tensor_tensor(out=var, in0=tmp, scalar=1.0 / D, in1=sq, op0=ALU.mult,
                                         op1=ALU.add).then_inc(s_var, 1)
                dve.wait_ge(s_sd, i + 1)
                link(dve.reciprocal(rstd, sd))
                for t in range(t0, t1):
                    ins = dve.tensor_scalar(xn[:, t, :], xn[:, t, :], small[:, 0, t:t + 1], small[:, 4, t:t + 1],
                                            ALU.subtract, ALU.mult)
                ins.then_inc(s_xn[i], 1)

            def max_unit(g, h):
                for c in range(CH):
                    dve.wait_ge(s_mxmm, 4 * HEADS * g + CH * h + c + 1)
                    dve.reduce_max(mx[:, c, h:h + 1], psM[:, c % 2, :], AX.X).then_inc(s_mx, 1)

            def split_max(g):
                part = [mparts[:, :, HEADS * i:HEADS * (i + 1)] for i in range(SPLITS)]
                dve.wait_ge(s_mx, 4 * HEADS * (g + 1))
                dve.tensor_scalar(part[0], mx[:, :, :], -1.0, None, ALU.mult).then_inc(s_mp, 1)
                dve.wait_ge(s_mp, 4 * g + 1)
                dve.scalar_tensor_tensor(out=mr[:, :, :], in0=mx[:, :, :], scalar=-1.0, in1=part[0], op0=ALU.mult,
                                         op1=ALU.subtract).then_inc(s_mp, 1)
                dve.wait_ge(s_mp, 4 * g + 2)
                dve.tensor_copy(part[1], mr[:, :, :]).then_inc(s_mp, 1)
                dve.wait_ge(s_mp, 4 * g + 3)
                dve.tensor_tensor(part[2], mr[:, :, :], part[1], ALU.subtract).then_inc(s_mp, 1)

            def step(kind, t, b, par):
                if kind == "xv_turn":
                    dve.wait_ge(s_xvt, b + 2)
                    dve.tensor_copy(xvT[:, :], psM[:, 0, :]).then_inc(s_xv, 1)
                elif kind == "max_turn":
                    dve.wait_ge(s_mt, b + 2)
                    if not (isinstance(b, int) and b < 0):
                        dve.wait_ge(s_mw, 16 * (b + 1))
                    dve.tensor_copy(mT[:, :], psMT[0:SPLITS * HEADS, :]).then_inc(s_mT, 1)
                elif kind == "v_proj":
                    dve.wait_ge(s_vp, b + 2)
                    v = v_s[1 - par][:, :, 0:9 * HEADS].rearrange("p c (h e) -> p c h e", e=9)[:, :, :, 0:HD]
                    dve.tensor_tensor(v, psM[:, 0, :].rearrange("p (c h e) -> p c h e", c=CH, e=HD),
                                      bv_s[:, None, :].to_broadcast([P, CH, D])
                                      .rearrange("p c (h e) -> p c h e", e=HD), ALU.add).then_inc(s_v, 1)
                elif kind in ("out0", "out1", "out2", "out3"):
                    c = int(kind[3])
                    src = (psV[:, :], psM[:, 1, :], psM[:, 0, :], psX[:, :])[c].rearrange("p (h e) -> p h e", e=32)
                    dve.wait_ge(s_outt, CH * b + c + 1)
                    dve.reciprocal(rden[:, c, :], src[:, :, HD]).then_inc(s_rd, 1)
                    dve.wait_ge(s_rd, CH * b + c + 1)
                    dve.tensor_tensor(att[:, c, :].rearrange("p (h e) -> p h e", e=HD), src[:, :, 0:HD],
                                      rden[:, c, :, None].to_broadcast([P, HEADS, HD]), ALU.mult).then_inc(s_norm, 1)
                elif kind == "wo":
                    dve.wait_ge(s_wo, b + 1)
                    dve.wait_ge(s_xb, b + 1)
                    if not (isinstance(b, int) and b >= MOE0):
                        scattered(b)
                    dve.tensor_tensor(xn[:, bass.ds(CH * b, CH), :], psM[:, 0, :].rearrange("p (c d) -> p c d", d=D),
                                      xres[:, :, :], ALU.add).then_inc(s_res, 1)
                elif kind == "slot_turn":
                    n = PER * (b - MOE0) + t
                    dve.wait_ge(s_xt, n + 1)
                    dve.tensor_copy(xT[t % 2][:, :], psS[:, 2, 0:SLOT]).then_inc(s_xT, 1)
                elif kind == "down":
                    n = PER * (b - MOE0) + t
                    dve.wait_ge(s_ym, n + 1)
                    dve.wait_ge(s_yst[t % 3], 16 * AHEAD + 16 * (PER // 3 * (b - MOE0) + t // 3))
                    w = w_e[t % 3][:, B3AT:B3AT + D]
                    dve.tensor_tensor(ys[t % 3][:, :, :], psS[:, 3, 0:2 * D].rearrange("p (c d) -> p c d", d=D),
                                      w[:, None, :].to_broadcast([P, 2, D]), ALU.add).then_inc(s_y, 1)

            def scattered(b):
                if is_moe[0]:
                    dve.wait_ge(s_scat, 2 * 16 * TILES)
                else:
                    dve.wait_ge(s_scat, 2 * 16 * 4 * CH * (b + 1))

            is_moe = [False]

            def route():
                logit, shifted, ex, w = work(0), work(1), work(2), work(3)
                v3 = lambda a: a.rearrange("p (t e) -> p t e", e=NE)
                tok = lambda a: a[:, :, None].to_broadcast([P, TILES, NE])
                per_e = lambda a: a[:, None, :].to_broadcast([P, TILES, NE])
                col = [work(10)[:, k * TILES:(k + 1) * TILES] for k in range(8)]
                dve.wait_ge(s_lread, 1)
                link(dve.tensor_reduce(col[0], v3(logit), AX.X, ALU.max))
                dve.tensor_tensor(v3(shifted), v3(logit), tok(col[0]), ALU.subtract).then_inc(s_gshift, 1)
                dve.wait_ge(s_gexp, 1)
                link(dve.tensor_reduce(col[1], v3(ex), AX.X, ALU.add))
                link(dve.reciprocal(col[2], col[1]))
                link(dve.tensor_tensor(v3(w), v3(ex), tok(col[2]), ALU.mult))
                picks = [work(4), work(5)]
                for k, gate in enumerate((gate1, gate2)):
                    link(dve.tensor_reduce(gate[:, :], v3(w), AX.X, ALU.max))
                    link(dve.tensor_tensor(v3(work(6)), v3(w), tok(gate[:, :]), ALU.is_equal))
                    link(dve.tensor_tensor(v3(work(6)), v3(work(6)), per_e(prio_s[:, :]), ALU.mult))
                    link(dve.tensor_reduce(col[3], v3(work(6)), AX.X, ALU.max))
                    link(dve.tensor_tensor(v3(picks[k]), v3(work(6)), tok(col[3]), ALU.is_equal))
                    if k == 0:
                        link(dve.scalar_tensor_tensor(out=w, in0=picks[0], scalar=-2.0, in1=w, op0=ALU.mult,
                                                      op1=ALU.add))
                dve.tensor_tensor(pair_b, picks[0], picks[1], ALU.add).then_inc(s_pick, 1)
                dve.wait_ge(s_rank, 1)
                in_tile, total = work(0), work(1)
                dve.tensor_copy(in_tile, psM[:, 0, :])
                dve.tensor_copy(total, psM[:, 1, :])
                dve.tensor_copy(work(2), psM[:, 1, :]).then_inc(s_ranked, 1)
                dve.wait_ge(s_ranked, 1)
                a, b_, n = work(2), work(3), 1
                while n < TILES:
                    dve.tensor_copy(b_[:, 0:n * NE], a[:, 0:n * NE])
                    link(dve.tensor_tensor(b_[:, n * NE:], a[:, n * NE:], a[:, :-n * NE], ALU.add))
                    a, b_, n = b_, a, 2 * n
                whole, ints = work(7), work(8).bitcast(I32)
                count = a[:, (TILES - 1) * NE:TILES * NE]
                link(dve.tensor_scalar(ints[:, 0:NE], count, float(SLOT - 1), None, ALU.add))
                link(dve.tensor_single_scalar(ints[:, NE:2 * NE], ints[:, 0:NE], SLOT.bit_length() - 1,
                                              ALU.logical_shift_right))
                link(dve.tensor_copy(whole[:, 0:NE], ints[:, NE:2 * NE]))
                dve.tensor_copy(whole[:, NE:2 * NE], whole[:, 0:NE])
                link(dve.tensor_tensor(work(6), a, total, ALU.subtract))
                p, r, n = NE, 2 * NE, 1
                while n < NE:
                    dve.tensor_copy(whole[:, r:r + n], whole[:, p:p + n])
                    link(dve.tensor_tensor(whole[:, r + n:r + NE], whole[:, p + n:p + NE], whole[:, p:p + NE - n],
                                           ALU.add))
                    p, r, n = r, r + NE, 2 * n
                end, base = whole[:, p:p + NE], whole[:, r:r + NE]
                link(dve.tensor_tensor(base, end, whole[:, 0:NE], ALU.subtract))
                link(dve.tensor_scalar(base, base, float(SLOT), None, ALU.mult))
                link(dve.tensor_tensor(work(6), work(6), in_tile, ALU.add))
                link(dve.tensor_tensor(v3(work(6)), v3(work(6)), per_e(base), ALU.add))
                for k in range(2):
                    link(dve.tensor_tensor(work(9), picks[k], work(6), ALU.mult))
                    link(dve.tensor_reduce(col[4 + k], v3(work(9)), AX.X, ALU.add))
                    link(dve.tensor_copy(slots[:, k, :], col[4 + k]))
                for t0 in range(0, ETILES, TILES):
                    t1 = min(ETILES, t0 + TILES)
                    c = work(9)[:, 0:(t1 - t0) * NE].rearrange("p (t e) -> p t e", e=NE)
                    link(dve.tensor_tensor(c, iota_s[:, t0:t1, None].to_broadcast([P, t1 - t0, NE]),
                                           end[:, None, :].to_broadcast([P, t1 - t0, NE]), ALU.is_ge))
                    link(dve.tensor_reduce(col[6][:, 0:t1 - t0], c, AX.X, ALU.add))
                    ins = dve.tensor_scalar(etile[:, t0:t1], col[6][:, 0:t1 - t0], float(NE - 1), None, ALU.min)
                    if t1 < ETILES:
                        link(ins)
                ins.then_inc(s_slots, 1)

            def combine(g):
                if g >= 2:
                    dve.wait_ge(s_out[g % 2], 16 * (g // 2))
                dve.wait_ge(s_gath[g % 2], 16 * 2 * CH * (g // 2 + 1))
                dve.wait_ge(s_res, AHEAD + g + 1)
                for k, gate in enumerate((gate1, gate2)):
                    for c in range(CH):
                        t = CH * g + c
                        before = xn[:, t, :] if k == 0 else outbuf[g % 2][:, c, :]
                        ins = dve.scalar_tensor_tensor(
                            out=outbuf[g % 2][:, c, :], in0=gathered[g % 2][:, CH * k + c, :],
                            scalar=gate[:, t:t + 1], in1=before, op0=ALU.mult, op1=ALU.add)
                    ins.then_inc((s_half, s_comb)[k], 1)
                    if k == 0:
                        dve.wait_ge(s_half, g + 1)

            layer_norm(0)
            step("xv_turn", None, -1, 1)
            step("v_proj", None, -1, 1)
            layer_norm(1)
            dve.wait_ge(s_logit, NB)
            dve.tensor_tensor(work(0).rearrange("p (t e) -> p t e", e=NE), psV[:, :].rearrange("p (t e) -> p t e", e=NE),
                              gb_s[:, None, :].to_broadcast([P, TILES, NE]), ALU.add).then_inc(s_lread, 1)
            for h in range(HEADS):
                max_unit(0, h)
            split_max(0)
            step("max_turn", None, -1, 1)
            route()

            def body(b, i, par, moe):
                is_moe[0] = moe
                late = list(combined(b))
                for u in range(UNITS):
                    if has_next(b):
                        max_unit(b + 1, u)
                    if u % 3 == 0 and u and late:
                        combine(late.pop(0))
                if has_next(b):
                    split_max(b + 1)
                for kind, t in between(b, moe):
                    step(kind, t, b, par)

            batches(dve, body)
            combine(NB - 1)


def kernel(**inputs):
    import numpy as np
    import concourse.bacc as bacc
    from concourse.bass_utils import run_bass_kernel_spmd

    get = lambda n: np.asarray(inputs[n])
    x = np.ascontiguousarray(get("L0_attn_x"))
    rows = get("L0_attn_Wqkv").reshape(HEADS, 3, HD, D)
    bias = get("L0_attn_bqkv").reshape(HEADS, 3, HD)
    w1, w2, w3 = get("L0_ffn_w1"), get("L0_ffn_w2"), get("L0_ffn_w3")
    b1, b2, b3 = get("L0_ffn_b1"), get("L0_ffn_b2"), get("L0_ffn_b3")
    wall = np.concatenate([
        w1,
        w2.reshape(NE, 2, P, HID).transpose(0, 2, 1, 3).reshape(NE, P, 2 * HID),
        w3.reshape(NE, 2, P, D).transpose(0, 2, 1, 3).reshape(NE, P, 2 * D),
        np.broadcast_to(b3[:, None, :], (NE, P, D)),
        b1.reshape(NE, 2, P).transpose(0, 2, 1),
        b2.reshape(NE, 2, P).transpose(0, 2, 1)], axis=2)
    arrays = {
        "x": x,
        "wq": rows[:, 0].reshape(P, D).T, "wk": rows[:, 1].reshape(P, D).T, "wv": rows[:, 2].reshape(P, D).T,
        "wo": get("L0_attn_Wo").T,
        "bq": bias[:, 0].reshape(P, 1), "bk": bias[:, 1].reshape(P, 1), "bv": bias[:, 2].reshape(P),
        "bo": get("L0_attn_bo"), "gate_w": get("L0_ffn_gate_w"), "gate_b": get("L0_ffn_gate_b"), "wall": wall,
        "ident": np.eye(P, dtype=np.float32), "tri": np.triu(np.ones((P, P), np.float32), 1),
        "iota": np.arange(ETILES, dtype=np.float32), "prio": np.arange(NE, 0, -1).astype(np.float32),
    }
    arrays = {n: np.ascontiguousarray(a) for n, a in arrays.items()}
    nc = bacc.Bacc("TRN2", target_bir_lowering=False, num_devices=1)
    args = [nc.dram_tensor(f"in_{n}", a.shape, F32, kind="ExternalInput").ap() for n, a in arrays.items()]
    out = nc.dram_tensor("out", x.shape, F32, kind="ExternalOutput").ap()
    build_block_kernel(nc, *args, out)
    result = run_bass_kernel_spmd(nc, [{f"in_{n}": a for n, a in arrays.items()}], core_ids=[0])
    return result.results[0]["out"]
```

```python
import concourse.bass as bass
from concourse import mybir
from contextlib import ExitStack

F32, BF16, I32, U32 = mybir.dt.float32, mybir.dt.bfloat16, mybir.dt.int32, mybir.dt.uint32
ALU, ACT, AX = mybir.AluOpType, mybir.ActivationFunctionType, mybir.AxisListType
P = 128
HEADS, HD = 16, 8
NB, SEQ, D = 16, 512, 128
CH = SEQ // P
TILES = NB * CH
NE, HID = 8, 256
SPLITS = 3
STACK = SPLITS * SPLITS * HD
SROWS = STACK + SPLITS
QUAD = 4
UNITS = HEADS // QUAD * CH
VW = 9 * HEADS + 24
SLOT = 256
ETILES = 72
WCOLS = HID + 2 * HID + 2 * D + D + 4
W2AT, W3AT, B3AT, BIAT = HID, 3 * HID, 3 * HID + 2 * D, 3 * HID + 3 * D
MOE0, MOE1, PER = 4, 12, 9
assert (MOE1 - MOE0) * PER == ETILES and ETILES * SLOT >= 2 * NB * SEQ + NE * (SLOT - 1)
EPS = 1e-5
SCALE = 1.0 / float(HD) ** 0.5


def build_block_kernel(nc, x, wq, wk, wv, wo, bq, bk, bv, bo, gate_w, gate_b, wall, ident, tri, iota, prio, out):
    with ExitStack() as ctx:
        def sb(name, shape, dt=F32):
            return ctx.enter_context(nc.sbuf_tensor(name, shape, dt))

        def sem(name):
            return ctx.enter_context(nc.semaphore(name))

        xn = sb("xn", [P, TILES, D])
        wq_s, wk_s, wv_s, wo_s = (sb(n, [P, P]) for n in ("wq_s", "wk_s", "wv_s", "wo_s"))
        bq_s, bk_s = sb("bq_s", [P, 1]), sb("bk_s", [P, 1])
        bv_s, bo_s = sb("bv_s", [P, D]), sb("bo_s", [P, D])
        gw_s, gb_s = sb("gw_s", [P, NE]), sb("gb_s", [P, NE])
        ident_s, ident_b = sb("ident_s", [P, P]), sb("ident_b", [P, P], BF16)
        prio_s, iota_s = sb("prio_s", [P, NE]), sb("iota_s", [P, ETILES])
        stats, small = sb("stats", [P, TILES, 6]), sb("small", [P, 6, TILES])
        gate1, gate2 = sb("gate1", [P, TILES]), sb("gate2", [P, TILES])
        slots = sb("slots", [P, 2, TILES], U32)
        etile = sb("etile", [P, ETILES], U32)
        xq_rows, xv_rows = sb("xq_rows", [P, CH, D]), sb("xv_rows", [P, CH, D])
        xqT, xvT = sb("xqT", [P, SEQ]), sb("xvT", [P, SEQ])
        qk_f, qk_r = sb("qk_f", [P, 2, SEQ]), sb("qk_r", [P, SEQ])
        parts = sb("parts", [P, 2, SPLITS, SEQ], BF16)
        qstack = [sb(f"qstack{i}", [P, HEADS, SEQ], BF16) for i in range(2)]
        kstack = [sb(f"kstack{i}", [P, HEADS, SEQ], BF16) for i in range(2)]
        v_s = [sb(f"v_s{i}", [P, CH, VW]) for i in range(2)]
        probs = sb("probs", [P, CH, QUAD, SEQ])
        mx, mr = sb("mx", [P, CH, HEADS]), sb("mr", [P, CH, HEADS])
        mparts = sb("mparts", [P, CH, SPLITS * HEADS], BF16)
        mT = sb("mT", [SPLITS * HEADS, SEQ], BF16)
        ot = sb("ot", [P, HEADS // QUAD, SEQ])
        rden, att = sb("rden", [P, CH, HEADS]), sb("att", [P, CH, D])
        attT, xres = sb("attT", [P, SEQ]), sb("xres", [P, CH, D])
        w_e = [sb(f"w_e{i}", [P, WCOLS]) for i in range(3)]
        xs = [sb(f"xs{i}", [P, 2, D]) for i in range(3)]
        ys = [sb(f"ys{i}", [P, 2, D]) for i in range(3)]
        xT = [sb(f"xT{i}", [P, SLOT]) for i in range(2)]
        h1, h2 = sb("h1", [P, 2, SLOT]), sb("h2", [P, 2, SLOT])
        ring = probs[:, :, :, :].rearrange("p a b c -> p (a b c)")

        def blocks(n, count):
            return ring[:, n * SEQ:(n + count) * SEQ]

        first_f = [qk_f] + [blocks(2 * g, 2).rearrange("p (s t) -> p s t", s=2) for g in range(2)]
        first_parts = [parts] + [blocks(4 + SPLITS * g, SPLITS).bitcast(BF16)
                                 .rearrange("p (s i t) -> p s i t", s=2, i=SPLITS) for g in range(2)]
        gate_xT = [blocks(10 + i, 1) for i in range(2)]
        flat = lambda a: a[:, :, :].rearrange("p c d -> p (c d)")
        wide = [w_e[i][:, k * SEQ:(k + 1) * SEQ] for i in range(3) for k in range(2)] + [flat(h2)]
        zeros = flat(h1)
        pair_b = flat(xs[0]).bitcast(BF16)
        tri_b, ones_b = flat(xs[1])[:, 0:64].bitcast(BF16), flat(xs[1])[:, 64:128].bitcast(BF16)
        tri_f = flat(xs[2])[:, 0:P]
        gathered = [w_e[i][:, 0:2 * CH * D].rearrange("p (k d) -> p k d", d=D) for i in range(2)]
        outbuf = [w_e[2][:, i * CH * D:(i + 1) * CH * D].rearrange("p (c d) -> p c d", d=D) for i in range(2)]

        psS = ctx.enter_context(nc.psum_tensor("psS", [P, 4, 512], F32))
        psM = ctx.enter_context(nc.psum_tensor("psM", [P, 2, 512], F32))
        psV = ctx.enter_context(nc.psum_tensor("psV", [P, 512], F32))
        psX = ctx.enter_context(nc.psum_tensor("psX", [P, 512], F32))
        psMT = psV[:, 0:256].bitcast(BF16)

        stack_d = nc.dram_tensor("stack_rows", [2, 2, HEADS, STACK, SEQ], BF16, kind="Internal").ap()
        max_d = nc.dram_tensor("max_rows", [2, SPLITS * HEADS, SEQ], BF16, kind="Internal").ap()
        xs_d = nc.dram_tensor("slot_rows", [ETILES * SLOT, D], F32, kind="Internal").ap()
        ys_d = nc.dram_tensor("slot_outs", [ETILES * SLOT, D], F32, kind="Internal").ap()
        xs_v = xs_d.rearrange("(n p c) d -> n p (c d)", p=P, c=2)
        ys_v = ys_d.rearrange("(n p c) d -> n p (c d)", p=P, c=2)
        x_v = x.rearrange("b (p c) d -> b p (c d)", c=CH)
        out_v = out.rearrange("b (p c) d -> b p (c d)", c=CH)

        s_const, s_zero, s_cst, s_zset = sem("s_const"), sem("s_zero"), sem("s_cst"), sem("s_zset")
        s_ones = sem("s_ones")
        ROWS = 16 * 2 * SPLITS
        CLEAR = 8 * P
        CONSTANTS = 16 * 14
        s_x = [sem(f"s_x{i}") for i in range(2)]
        s_dve = sem("s_dve")
        s_var, s_sd = sem("s_var"), sem("s_sd")
        s_xn = [sem(f"s_xn{i}") for i in range(2)]
        s_gxt, s_gx, s_logit = sem("s_gxt"), sem("s_gx"), sem("s_logit")
        s_lread = sem("s_lread")
        s_gshift, s_gexp = sem("s_gshift"), sem("s_gexp")
        s_pick, s_rank, s_ranked, s_slots = sem("s_pick"), sem("s_rank"), sem("s_ranked"), sem("s_slots")
        s_xqrow, s_xqt, s_xq = sem("s_xqrow"), sem("s_xqt"), sem("s_xq")
        s_xvrow, s_xvt, s_xv = sem("s_xvrow"), sem("s_xvt"), sem("s_xv")
        s_qp, s_kp, s_qf, s_kf = sem("s_qp"), sem("s_kp"), sem("s_qf"), sem("s_kf")
        s_part, s_rows = sem("s_part"), sem("s_rows")
        s_stack = [[sem(f"s_stack{i}{q}") for q in range(HEADS // QUAD)] for i in range(2)]
        s_vp, s_v = sem("s_vp"), sem("s_v")
        s_mxmm, s_mx, s_mp = sem("s_mxmm"), sem("s_mx"), sem("s_mp")
        s_mt, s_mT, s_mw, s_mrow = sem("s_mt"), sem("s_mT"), sem("s_mw"), sem("s_mrow")
        s_st, s_exp, s_pvu, s_ot = sem("s_st"), sem("s_exp"), sem("s_pvu"), sem("s_ot")
        s_outt, s_rd, s_norm = sem("s_outt"), sem("s_rd"), sem("s_norm")
        s_att, s_attT, s_wo = sem("s_att"), sem("s_attT"), sem("s_wo")
        s_xres, s_xb, s_res = sem("s_xres"), sem("s_xb"), sem("s_res")
        s_scat = sem("s_scat")
        s_w = [sem(f"s_w{i}") for i in range(3)]
        s_xs = [sem(f"s_xs{i}") for i in range(3)]
        s_yst = [sem(f"s_yst{i}") for i in range(3)]
        s_xt, s_xT, s_h1m, s_h1 = sem("s_xt"), sem("s_xT"), sem("s_h1m"), sem("s_h1")
        s_h2m, s_h2, s_ym, s_y = sem("s_h2m"), sem("s_h2"), sem("s_ym"), sem("s_y")
        s_gath = [sem(f"s_gath{i}") for i in range(2)]
        s_out = [sem(f"s_out{i}") for i in range(2)]
        AHEAD = 1
        s_half, s_comb = sem("s_half"), sem("s_comb")
        s_settled = sem("s_settled")

        AUX = ["pv_last", "xq_turn", "xv_turn", "max_turn", "q_proj", "v_proj", "k_proj",
               "out0", "out1", "out2", "out3", "att_turn", "wo"]

        def between(b, moe):
            aux = [(a, None) for a in AUX]
            if isinstance(b, int) and b + 3 >= NB:
                aux = [a for a in aux if a[0] not in ("xq_turn", "q_proj", "k_proj")]
            if isinstance(b, int) and b + 1 >= NB:
                aux = [a for a in aux if a[0] not in ("xv_turn", "max_turn", "v_proj")]
            if not moe:
                return aux
            steps = [aux.pop(0), ("slot_turn", 0), aux.pop(0), ("slot_turn", 1), ("up", 0), aux.pop(0), aux.pop(0)]
            for t in range(PER):
                steps.append(("mid", t))
                if t + 1 < PER:
                    steps.append(("up", t + 1))
                if t + 2 < PER:
                    steps.append(("slot_turn", t + 2))
                steps += [aux.pop(0)] if aux else []
                steps.append(("down", t))
            return steps + aux

        def settle(eng):
            eng.sem_inc(s_settled, 1)

        def has_qk(b):
            return not isinstance(b, int) or b + 3 < NB

        def has_next(b):
            return not isinstance(b, int) or b + 1 < NB

        COMBINED = {12: range(0, 5), 13: range(5, 10), 14: range(10, 14), 15: range(14, 15)}

        def combined(b):
            return COMBINED.get(b, range(0)) if isinstance(b, int) else range(0)

        def batches(eng, body, loop_first=True):
            if loop_first:
                with eng.Fori(0, MOE0 // 2) as i:
                    for par in range(2):
                        body(2 * i + par, i, par, False)
            else:
                for b in range(MOE0):
                    body(b, b // 2, b % 2, False)
            with eng.Fori(MOE0 // 2, MOE1 // 2) as i:
                for par in range(2):
                    body(2 * i + par, i, par, True)
            for b in range(MOE1, NB):
                body(b, b // 2, b % 2, False)

        block = ctx.enter_context(nc.Block())

        @block.sync
        def _(sp):
            for dst, src in ((xn[:, 0:2 * CH, :].rearrange("p (b c) d -> p b (c d)", c=CH), x_v[0:2]),
                             (xn[:, 2 * CH:4 * CH, :].rearrange("p (b c) d -> p b (c d)", c=CH), x_v[2:4])):
                sp.dma_start(dst, src.rearrange("b p k -> p b k")).then_inc(s_x[0], 16)
            for dst, src in ((ident_s[:, :], ident), (wq_s[:, :], wq), (wk_s[:, :], wk), (wv_s[:, :], wv),
                             (wo_s[:, :], wo), (bq_s[:, :], bq), (bk_s[:, :], bk),
                             (bv_s[:, :], bv.partition_broadcast(P)), (bo_s[:, :], bo.partition_broadcast(P)),
                             (gw_s[:, :], gate_w), (gb_s[:, :], gate_b.partition_broadcast(P)),
                             (prio_s[:, :], prio.partition_broadcast(P)), (iota_s[:, :], iota.partition_broadcast(P)),
                             (tri_f, tri)):
                sp.dma_start(dst, src).then_inc(s_const, 16)
            for b in range(4, NB, 2):
                sp.dma_start(xn[:, CH * b:CH * (b + 2), :].rearrange("p (b c) d -> p b (c d)", c=CH),
                             x_v[b:b + 2].rearrange("b p k -> p b k")).then_inc(s_x[1], 16)

            def clear(first, last):
                for r in range(first * CLEAR, last * CLEAR, CLEAR):
                    sp.dma_start(xs_d[r:r + CLEAR, :].rearrange("(p r) d -> p (r d)", p=P)
                                 .rearrange("p (i k) -> p i k", i=2),
                                 zeros[:, None, :].to_broadcast([P, 2, SEQ])).then_inc(s_zero, 16)

            def write_rows(g, pair, par, parts=parts):
                sp.wait_ge(s_part, 8 * (g + 1))
                settle(sp)
                if not isinstance(g, int) or g >= 2:
                    for q in range(HEADS // QUAD):
                        sp.wait_ge(s_stack[par][q], 32 * pair)
                for i in range(SPLITS):
                    for side in range(2):
                        rows = stack_d[side, par].rearrange("h (d i j) t -> i j (h d) t", i=SPLITS, j=SPLITS)
                        for_part = rows[i] if side == 0 else rows[:, i]
                        sp.dma_start(for_part.rearrange("n p t -> p n t"),
                                     parts[:, side, i, None, :].to_broadcast([P, SPLITS, SEQ])) \
                            .then_inc(s_rows, 16)

            def read_rows(par, q):
                for side, stack in ((0, qstack), (1, kstack)):
                    sp.dma_start(stack[par][0:STACK, QUAD * q:QUAD * (q + 1), :],
                                 stack_d[side, par, QUAD * q:QUAD * (q + 1)].rearrange("h r t -> r h t")).then_inc(s_stack[par][q], 16)

            def write_max(g, par):
                sp.wait_ge(s_mT, g + 1)
                sp.dma_start(max_d[par], mT[:, :]).then_inc(s_mw, 16)

            def read_max(g, par):
                sp.wait_ge(s_mw, 16 * (g + 1))
                sp.dma_start(qstack[par][STACK:SROWS, :, :],
                             max_d[par].rearrange("(s h) t -> s h t", s=SPLITS)).then_inc(s_mrow, 16)

            def expert_of(n):
                return sp.value_load(etile[0:1, bass.ds(n, 1)], min_val=0, max_val=NE - 1)

            def load_weights(e, t):
                sp.dma_start(w_e[t % 3][:, :], wall[bass.ds(e, 1)].rearrange("e p n -> (e p) n")) \
                    .then_inc(s_w[t % 3], 16)

            def load_rows(n, t):
                sp.dma_start(xs[t % 3][:, :, :].rearrange("p c d -> p (c d)"),
                             xs_v[bass.ds(n, 1)].rearrange("n p k -> (n p) k")).then_inc(s_xs[t % 3], 16)

            sp.wait_ge(s_zset, 1)
            clear(0, 6)
            for g in range(3):
                write_rows(g, g // 2, g % 2, first_parts[g])
                if g < 2:
                    sp.wait_ge(s_rows, ROWS * (g + 1))
                    sp.wait_ge(s_ones, 2 * (g + 1))
                    for q in range(HEADS // QUAD):
                        read_rows(g, q)
                clear((6, 8, 10)[g], (8, 10, 18)[g])
            write_max(0, 0)
            read_max(0, 0)

            def body(b, i, par, moe):
                late = list(combined(b))
                if has_qk(b):
                    if not moe:
                        sp.wait_ge(s_xn[1], 1)
                    sp.wait_ge(s_xqt, b + 3)
                    sp.dma_start(xq_rows[:, :, :], xn[:, bass.ds(CH * (b + 3), CH), :]).then_inc(s_xqrow, 16)
                if has_next(b):
                    sp.wait_ge(s_xvt, b + 1)
                    sp.dma_start(xv_rows[:, :, :], xn[:, bass.ds(CH * (b + 1), CH), :]).then_inc(s_xvrow, 16)
                sp.wait_ge(s_res, AHEAD + b)
                sp.dma_start(xres[:, :, :].rearrange("p c d -> p (c d)"),
                             x_v[bass.ds(b, 1)].rearrange("b p k -> (b p) k")).then_inc(s_xres, 16)
                if moe:
                    sp.wait_ge(s_scat, 2 * 16 * TILES)
                    sp.wait_ge(s_y, AHEAD + PER * (b - MOE0))
                    settle(sp)
                    for t in range(3):
                        n = PER * (b - MOE0) + t
                        load_rows(n, t)
                        load_weights(expert_of(n), t)
                if not isinstance(b, int) or b + 2 < NB:
                    sp.wait_ge(s_rows, ROWS * (b + 3))
                    for q in range(HEADS // QUAD):
                        sp.wait_ge(s_st, 2 * UNITS * b + 2 * CH * (q + 1))
                        read_rows(par, q)
                        if late:
                            store_out(late.pop(0))
                for g in late:
                    store_out(g)
                if has_next(b):
                    write_max(b + 1, 1 - par)
                    if not moe:
                        read_max(b + 1, 1 - par)
                for t in range(PER if moe else 0):
                    n = PER * (b - MOE0) + t
                    if t + 3 < PER:
                        sp.wait_ge(s_xt, n + 1)
                        load_rows(n + 3, t)
                        settle(sp)
                        e = expert_of(n + 3)
                    sp.wait_ge(s_y, AHEAD + n + 1)
                    if t + 3 < PER:
                        load_weights(e, t)
                    sp.dma_start(ys_v[bass.ds(n, 1)].rearrange("n p k -> (n p) k"),
                                 ys[t % 3][:, :, :].rearrange("p c d -> p (c d)")).then_inc(s_yst[t % 3], 16)
                    if t == 0:
                        read_max(b + 1, 1 - par)
                if has_qk(b):
                    write_rows(b + 3, i + (par + 3) // 2, 1 - par)

            def store_out(g):
                sp.wait_ge(s_comb, g + 1)
                sp.dma_start(out_v[g], outbuf[g % 2].rearrange("p c d -> p (c d)")).then_inc(s_out[g % 2], 16)

            batches(sp, body)
            store_out(NB - 1)
            for i in range(2):
                sp.wait_ge(s_out[i], 16 * NB // 2)

        @block.gpsimd
        def _(pool):
            def split(g, qk_f=qk_f, parts=parts, first=False):
                if not first:
                    pool.wait_ge(s_rows, ROWS * g)
                for side, s_f in ((0, s_qf), (1, s_kf)):
                    pool.wait_ge(s_f, g + 1)
                    settle(pool)
                    f, part = qk_f[:, side, :], [parts[:, side, i, :] for i in range(SPLITS)]
                    at = 8 * g + 4 * side
                    pool.tensor_scalar(part[0], f, 1.0, 0.0, ALU.mult, ALU.add).then_inc(s_part, 1)
                    pool.wait_ge(s_part, at + 1)
                    pool.tensor_tensor(qk_r[:, :], f, part[0], ALU.subtract).then_inc(s_part, 1)
                    pool.wait_ge(s_part, at + 2)
                    settle(pool)
                    pool.tensor_scalar(part[1], qk_r[:, :], 1.0, 0.0, ALU.mult, ALU.add).then_inc(s_part, 1)
                    pool.wait_ge(s_part, at + 3)
                    pool.tensor_tensor(part[2], qk_r[:, :], part[1], ALU.subtract).then_inc(s_part, 1)
                    pool.wait_ge(s_part, at + 4)

            def scatter(g):
                for t in range(CH * g, CH * (g + 1)):
                    for k in range(2):
                        pool.indirect_dma_start(
                            out=xs_d, out_offset=bass.IndirectOffsetOnAxis(ap=slots[:, k, t:t + 1], axis=0),
                            in_=xn[:, t, :], in_offset=None).then_inc(s_scat, 16)

            def gather(g):
                if g >= 2:
                    pool.wait_ge(s_comb, g - 1)
                for k in range(2):
                    for c in range(CH):
                        t = CH * g + c
                        pool.indirect_dma_start(
                            out=gathered[g % 2][:, CH * k + c, :], out_offset=None, in_=ys_d,
                            in_offset=bass.IndirectOffsetOnAxis(ap=slots[:, k, t:t + 1], axis=0)) \
                            .then_inc(s_gath[g % 2], 16)

            pool.memset(zeros, 0.0).then_inc(s_zset, 1)
            pool.wait_ge(s_zset, 1)
            pool.memset(v_s[0][:, :, :], 1.0).then_inc(s_ones, 1)
            pool.wait_ge(s_ones, 1)
            pool.memset(kstack[0][64:96, :, :], 1.0).then_inc(s_ones, 1)
            pool.wait_ge(s_ones, 2)
            for g in range(3):
                split(g, first_f[g], first_parts[g], True)
                if g == 0:
                    pool.memset(kstack[1][64:96, :, :], 1.0).then_inc(s_ones, 1)
                    pool.wait_ge(s_ones, 3)
                    pool.memset(v_s[1][:, :, :], 1.0).then_inc(s_ones, 1)
                    pool.wait_ge(s_ones, 4)

            def body(b, i, par, moe):
                if isinstance(b, int) and b < MOE0:
                    if b == 0:
                        pool.wait_ge(s_slots, 1)
                        pool.wait_ge(s_zero, 16 * ETILES * SLOT // CLEAR)
                        pool.wait_ge(s_xn[1], 1)
                    else:
                        pool.wait_ge(s_res, AHEAD + b)
                    for g in range(4 * b, 4 * b + 4):
                        scatter(g)
                for g in combined(b):
                    if g == 0:
                        for i in range(3):
                            pool.wait_ge(s_yst[i], 16 * AHEAD + 16 * ETILES // 3)
                    gather(g)
                pool.wait_ge(s_xres, 16 * (b + 1))
                pool.tensor_tensor(xres[:, :, :], xres[:, :, :], bo_s[:, None, :].to_broadcast([P, CH, D]),
                                   ALU.add).then_inc(s_xb, 1)
                if has_qk(b):
                    split(b + 3)

            pool.wait_ge(s_const, CONSTANTS)
            batches(pool, body, loop_first=False)
            gather(NB - 1)

        @block.scalar
        def _(act):
            def deviation(i):
                act.wait_ge(s_var, i + 1)
                t0, t1 = ((0, 16), (16, TILES))[i]
                act.activation(small[:, 3, t0:t1], small[:, 2, t0:t1], ACT.Sqrt).then_inc(s_sd, 1)

            def step(kind, t, b):
                if kind == "pv_last":
                    act.wait_ge(s_pvu, UNITS * (b + 1))
                    act.activation(ot[:, 3, :], psV[:, :], ACT.Copy).then_inc(s_ot, 1)
                elif kind == "xq_turn":
                    act.wait_ge(s_xqt, b + 4)
                    act.activation(xqT[:, :], psX[:, :], ACT.Copy).then_inc(s_xq, 1)
                elif kind == "q_proj":
                    act.wait_ge(s_qp, b + 4)
                    act.wait_ge(s_part, 8 * (b + 3))
                    act.activation(qk_f[:, 0, :], psM[:, 1, :], ACT.Identity, bias=bq_s[:, 0:1]).then_inc(s_qf, 1)
                elif kind == "k_proj":
                    act.wait_ge(s_kp, b + 4)
                    act.activation(qk_f[:, 1, :], psX[:, :], ACT.Identity, bias=bk_s[:, 0:1]).then_inc(s_kf, 1)
                elif kind == "att_turn":
                    act.wait_ge(s_att, b + 1)
                    act.activation(attT[:, :], psM[:, 1, :], ACT.Copy).then_inc(s_attT, 1)
                elif kind in ("up", "mid"):
                    n = PER * (b - MOE0) + t
                    mm, done, bank, dst, at = (s_h1m, s_h1, 0, h1, BIAT) if kind == "up" else \
                        (s_h2m, s_h2, 1, h2, BIAT + 2)
                    act.wait_ge(mm, n + 1)
                    for c in range(2):
                        act.activation(dst[:, c, :], psS[:, bank, c * SLOT:(c + 1) * SLOT], ACT.Gelu,
                                       bias=w_e[t % 3][:, at + c:at + c + 1]).then_inc(done, 1)

            act.wait_ge(s_const, CONSTANTS)
            deviation(0)
            for g in range(3):
                act.wait_ge(s_xqt, g + 1)
                if g == 1:
                    act.wait_ge(s_vp, 1)
                act.activation(xqT[:, :], psS[:, g, :], ACT.Copy).then_inc(s_xq, 1)
                act.wait_ge(s_qp, g + 1)
                act.activation(first_f[g][:, 0, :], psM[:, 1, :], ACT.Identity, bias=bq_s[:, 0:1]).then_inc(s_qf, 1)
                act.wait_ge(s_kp, g + 1)
                act.activation(first_f[g][:, 1, :], psX[:, :], ACT.Identity, bias=bk_s[:, 0:1]).then_inc(s_kf, 1)
            deviation(1)
            for g in range(NB):
                act.wait_ge(s_gxt, g + 1)
                if g >= 2:
                    act.wait_ge(s_logit, g - 1)
                act.activation(gate_xT[g % 2], psS[:, g % 4, :], ACT.Copy).then_inc(s_gx, 1)
            act.wait_ge(s_gshift, 1)
            act.activation(wide[2], wide[1], ACT.Exp).then_inc(s_gexp, 1)
            act.wait_ge(s_logit, NB)
            act.wait_ge(s_rows, 3 * ROWS)

            def body(b, i, par, moe):
                for u in range(UNITS):
                    for half in range(2):
                        act.wait_ge(s_st, 2 * UNITS * b + 2 * u + half + 1)
                        if u >= CH and half == 0:
                            act.wait_ge(s_pvu, UNITS * b + u - CH + 1)
                        act.activation(probs[:, u % CH, 2 * half:2 * half + 2, :],
                                       psS[:, 2 * half:2 * half + 2, :], ACT.Exp, scale=SCALE).then_inc(s_exp, 1)
                    if u % CH == 0 and u:
                        q = u // CH - 1
                        act.wait_ge(s_pvu, UNITS * b + CH * (q + 1))
                        act.activation(ot[:, q, :], psV[:, :], ACT.Copy).then_inc(s_ot, 1)
                for kind, t in between(b, moe):
                    step(kind, t, b)

            batches(act, body)

        @block.tensor
        def _(pe):
            def turn_rows(dst, rows, done):
                for c in range(CH):
                    mm = pe.transpose(dst[:, c * P:(c + 1) * P], rows[:, c, :], ident_s[:, :])
                mm.then_inc(done, 1)

            def max_unit(g, pair, par, h, chunks):
                if h % QUAD == 0 and chunks[0] == 0:
                    pe.wait_ge(s_stack[par][h // QUAD], 32 * (pair + 1))
                for c in chunks:
                    i = CH * h + c
                    if i >= 2:
                        pe.wait_ge(s_mx, 4 * HEADS * g + i - 1)
                    pe.matmul(psM[:, i % 2, :], qstack[par][0:STACK, h, c * P:(c + 1) * P],
                              kstack[par][0:STACK, h, :], start=True, stop=True).then_inc(s_mxmm, 1)

            def pv_unit(b, par, u):
                q, kc = u // CH, u % CH
                pe.wait_ge(s_exp, 2 * UNITS * b + 2 * u + 2)
                if kc == 0 and q:
                    pe.wait_ge(s_ot, 4 * b + q)
                if u == 0:
                    pe.wait_ge(s_v, b + 1)
                for j in range(QUAD):
                    h = QUAD * q + j
                    mm = pe.matmul(psV[32 * j:32 * (j + 1), :], v_s[par][:, kc, 9 * h:9 * h + 32],
                                   probs[:, u % CH, j, :], start=(kc == 0), stop=(kc == CH - 1),
                                   tile_position=(0, 32 * j))
                mm.then_inc(s_pvu, 1)
                return mm

            def step(kind, t, b, par):
                if kind == "pv_last":
                    pv_unit(b, par, UNITS - 1)
                elif kind == "xq_turn":
                    pe.wait_ge(s_xqrow, 16 * (b + 1))
                    turn_rows(psX, xq_rows, s_xqt)
                elif kind == "xv_turn":
                    pe.wait_ge(s_xvrow, 16 * (b + 1))
                    pe.wait_ge(s_mx, 4 * HEADS * (b + 2))
                    turn_rows(psM[:, 0, :], xv_rows, s_xvt)
                elif kind == "max_turn":
                    pe.wait_ge(s_mp, 4 * (b + 2))
                    if not (isinstance(b, int) and b < 0):
                        pe.wait_ge(s_ot, 4 * b + 4)
                    settle(pe)
                    for c in range(CH):
                        mm = pe.transpose(psMT[0:SPLITS * HEADS, c * P:(c + 1) * P], mparts[:, c, :], ident_b[:, :])
                    mm.then_inc(s_mt, 1)
                elif kind == "q_proj":
                    pe.wait_ge(s_xq, b + 4)
                    pe.matmul(psM[:, 1, :], wq_s[:, :], xqT[:, :], start=True, stop=True).then_inc(s_qp, 1)
                elif kind == "k_proj":
                    pe.matmul(psX[:, :], wk_s[:, :], xqT[:, :], start=True, stop=True).then_inc(s_kp, 1)
                elif kind == "v_proj":
                    pe.wait_ge(s_xv, b + 2)
                    for c in range(CH):
                        mm = pe.matmul(psM[:, 0, c * P:(c + 1) * P], xvT[:, c * P:(c + 1) * P], wv_s[:, :],
                                       start=True, stop=True)
                    mm.then_inc(s_vp, 1)
                elif kind in ("out0", "out1", "out2", "out3"):
                    c = int(kind[3])
                    if c == 0:
                        pe.wait_ge(s_ot, 4 * b + 4)
                        if has_next(b):
                            pe.wait_ge(s_mT, b + 2)
                    elif c == 1 and has_qk(b):
                        pe.wait_ge(s_qf, b + 4)
                    elif c == 1 and has_next(b):
                        pe.wait_ge(s_mx, 4 * HEADS * (b + 2))
                    elif c == 2 and has_next(b):
                        pe.wait_ge(s_v, b + 2)
                    elif c == 2:
                        pe.wait_ge(s_res, AHEAD + b)
                    elif c == 3 and has_qk(b):
                        pe.wait_ge(s_kf, b + 4)
                    dst = (psV[:, :], psM[:, 1, :], psM[:, 0, :], psX[:, :])[c]
                    for q in range(HEADS // QUAD):
                        mm = pe.transpose(dst[:, q * P:(q + 1) * P], ot[:, q, c * P:(c + 1) * P], ident_s[:, :])
                    mm.then_inc(s_outt, 1)
                elif kind == "att_turn":
                    pe.wait_ge(s_norm, CH * (b + 1))
                    turn_rows(psM[:, 1, :], att, s_att)
                elif kind == "wo":
                    pe.wait_ge(s_attT, b + 1)
                    for c in range(CH):
                        mm = pe.matmul(psM[:, 0, c * P:(c + 1) * P], attT[:, c * P:(c + 1) * P], wo_s[:, :],
                                       start=True, stop=True)
                    mm.then_inc(s_wo, 1)
                else:
                    n, w = PER * (b - MOE0) + t, w_e[t % 3]
                    third = 16 * (PER // 3 * (b - MOE0) + t // 3 + 1)
                    if kind == "slot_turn":
                        pe.wait_ge(s_xs[t % 3], third)
                        if t:
                            pe.wait_ge(s_xT, n)
                        for c in range(2):
                            mm = pe.transpose(psS[:, 2, c * P:(c + 1) * P], xs[t % 3][:, c, :], ident_s[:, :])
                        mm.then_inc(s_xt, 1)
                    elif kind == "up":
                        pe.wait_ge(s_w[t % 3], third)
                        pe.wait_ge(s_xT, n + 1)
                        if t:
                            pe.wait_ge(s_h1, 2 * n)
                        for c in range(2):
                            mm = pe.matmul(psS[:, 0, c * SLOT:(c + 1) * SLOT], w[:, c * P:(c + 1) * P],
                                           xT[t % 2][:, :], start=True, stop=True)
                        mm.then_inc(s_h1m, 1)
                    elif kind == "mid":
                        pe.wait_ge(s_h1, 2 * n + 2)
                        if t:
                            pe.wait_ge(s_h2, 2 * n)
                        for c in range(2):
                            for k in range(2):
                                at = W2AT + k * HID + c * P
                                mm = pe.matmul(psS[:, 1, c * SLOT:(c + 1) * SLOT], w[:, at:at + P], h1[:, k, :],
                                               start=(k == 0), stop=(k == 1))
                        mm.then_inc(s_h2m, 1)
                    elif kind == "down":
                        pe.wait_ge(s_h2, 2 * n + 2)
                        if t:
                            pe.wait_ge(s_y, AHEAD + n)
                        for c in range(2):
                            for k in range(2):
                                at = W3AT + k * D
                                mm = pe.matmul(psS[:, 3, c * P:(c + 1) * P], h2[:, k, c * P:(c + 1) * P],
                                               w[:, at:at + D], start=(k == 0), stop=(k == 1))
                        mm.then_inc(s_ym, 1)

            pe.wait_ge(s_const, CONSTANTS)
            pe.wait_ge(s_cst, 1)
            pe.sem_inc(s_xvt, AHEAD)
            pe.wait_ge(s_xn[0], 1)
            for g in range(3):
                turn_rows(psS[:, g, :], xn[:, CH * g:CH * (g + 1), :], s_xqt)
            for g in range(3):
                pe.wait_ge(s_xq, g + 1)
                if g:
                    pe.wait_ge(s_qf, g)
                pe.matmul(psM[:, 1, :], wq_s[:, :], xqT[:, :], start=True, stop=True).then_inc(s_qp, 1)
                if g:
                    pe.wait_ge(s_kf, g)
                pe.matmul(psX[:, :], wk_s[:, :], xqT[:, :], start=True, stop=True).then_inc(s_kp, 1)
                if g == 0:
                    for c in range(CH):
                        mm = pe.matmul(psM[:, 0, c * P:(c + 1) * P], xqT[:, c * P:(c + 1) * P], wv_s[:, :],
                                       start=True, stop=True)
                    mm.then_inc(s_vp, 1)

            def gate(g):
                if g < NB:
                    if g == 4:
                        pe.wait_ge(s_xn[1], 1)
                    if g >= 4:
                        pe.wait_ge(s_gx, g - 3)
                    turn_rows(psS[:, g % 4, :], xn[:, CH * g:CH * (g + 1), :], s_gxt)
                if g:
                    pe.wait_ge(s_gx, g)
                    for c in range(CH):
                        at = NE * (CH * (g - 1) + c)
                        mm = pe.matmul(psV[:, at:at + NE], gate_xT[(g - 1) % 2][:, c * P:(c + 1) * P], gw_s[:, :],
                                       start=True, stop=True)
                    mm.then_inc(s_logit, 1)

            pe.wait_ge(s_v, 1)
            pe.wait_ge(s_qf, 3)
            for h in range(HEADS):
                gate(h)
                max_unit(0, 0, 0, h, range(CH))
            gate(NB)
            pe.wait_ge(s_lread, 1)
            step("max_turn", None, -1, 1)
            pe.wait_ge(s_pick, 1)
            for i, m in enumerate((tri_b, ones_b)):
                mm = pe.matmul(psM[:, i, :], m, pair_b, start=True, stop=True)
            mm.then_inc(s_rank, 1)
            pe.wait_ge(s_ranked, 1)
            pe.wait_ge(s_mT, 1)

            def body(b, i, par, moe):
                if moe:
                    pe.wait_ge(s_y, AHEAD + PER * (b - MOE0))
                elif isinstance(b, int):
                    pe.wait_ge(s_y, AHEAD + ETILES)
                pe.wait_ge(s_res, AHEAD + b)
                pe.wait_ge(s_mrow, 16 * (b + 1))
                for u in range(UNITS):
                    q, kc = u // CH, u % CH
                    for half in range(2):
                        if u:
                            pe.wait_ge(s_exp, 2 * UNITS * b + 2 * u + half - 1)
                        for j in range(2 * half, 2 * half + 2):
                            h = QUAD * q + j
                            mm = pe.matmul(psS[:, j, :], kstack[par][0:SROWS, h, kc * P:(kc + 1) * P],
                                           qstack[par][0:SROWS, h, :], start=True, stop=True)
                        mm.then_inc(s_st, 1)
                    if has_next(b):
                        max_unit(b + 1, i + (par + 1) // 2, 1 - par, u, range(0, 2))
                    if u:
                        mm = pv_unit(b, par, u - 1)
                    if has_next(b):
                        max_unit(b + 1, i + (par + 1) // 2, 1 - par, u, range(2, CH))
                for kind, t in between(b, moe):
                    step(kind, t, b, par)

            batches(pe, body)

        @block.vector
        def _(dve):
            done = [0]

            def link(ins):
                done[0] += 1
                ins.then_inc(s_dve, 1)
                dve.wait_ge(s_dve, done[0])

            dve.sem_inc(s_res, AHEAD)
            dve.sem_inc(s_y, AHEAD)
            for place in s_yst:
                dve.sem_inc(place, 16 * AHEAD)
            dve.sem_inc(s_xv, AHEAD)
            dve.wait_ge(s_const, CONSTANTS)
            dve.tensor_copy(ident_b[:, :], ident_s[:, :])
            dve.tensor_copy(tri_b, tri_f)
            dve.memset(ones_b, 1.0).then_inc(s_cst, 1)

            def layer_norm(i):
                t0, t1 = ((0, 16), (16, TILES))[i]
                dve.wait_ge(s_x[i], 16 * (2, 6)[i])
                for t in range(t0, t1):
                    ins = dve.bn_stats(stats[:, t, :], xn[:, t, :])
                link(ins)
                st = stats[:, t0:t1, :]
                mean, tmp, var, sd, rstd, sq = (small[:, k, t0:t1] for k in range(6))
                dve.tensor_tensor(sq, st[:, :, 1], st[:, :, 4], ALU.subtract)
                dve.tensor_tensor(tmp, st[:, :, 2], st[:, :, 5], ALU.add)
                link(dve.tensor_tensor(mean, st[:, :, 1], st[:, :, 4], ALU.add))
                dve.tensor_scalar(mean, mean, 0.5, None, ALU.mult)
                link(dve.tensor_tensor(sq, sq, sq, ALU.mult))
                link(dve.tensor_scalar(sq, sq, 0.25, EPS, ALU.mult, ALU.add))
                dve.scalar_tensor_tensor(out=var, in0=tmp, scalar=1.0 / D, in1=sq, op0=ALU.mult,
                                         op1=ALU.add).then_inc(s_var, 1)
                dve.wait_ge(s_sd, i + 1)
                link(dve.reciprocal(rstd, sd))
                for t in range(t0, t1):
                    ins = dve.tensor_scalar(xn[:, t, :], xn[:, t, :], small[:, 0, t:t + 1], small[:, 4, t:t + 1],
                                            ALU.subtract, ALU.mult)
                ins.then_inc(s_xn[i], 1)

            def max_unit(g, h):
                for c in range(CH):
                    dve.wait_ge(s_mxmm, 4 * HEADS * g + CH * h + c + 1)
                    dve.reduce_max(mx[:, c, h:h + 1], psM[:, c % 2, :], AX.X).then_inc(s_mx, 1)

            def split_max(g):
                part = [mparts[:, :, HEADS * i:HEADS * (i + 1)] for i in range(SPLITS)]
                dve.wait_ge(s_mx, 4 * HEADS * (g + 1))
                dve.tensor_scalar(part[0], mx[:, :, :], -1.0, None, ALU.mult).then_inc(s_mp, 1)
                dve.wait_ge(s_mp, 4 * g + 1)
                dve.scalar_tensor_tensor(out=mr[:, :, :], in0=mx[:, :, :], scalar=-1.0, in1=part[0], op0=ALU.mult,
                                         op1=ALU.subtract).then_inc(s_mp, 1)
                dve.wait_ge(s_mp, 4 * g + 2)
                dve.tensor_copy(part[1], mr[:, :, :]).then_inc(s_mp, 1)
                dve.wait_ge(s_mp, 4 * g + 3)
                dve.tensor_tensor(part[2], mr[:, :, :], part[1], ALU.subtract).then_inc(s_mp, 1)

            def step(kind, t, b, par):
                if kind == "xv_turn":
                    dve.wait_ge(s_xvt, b + 2)
                    dve.tensor_copy(xvT[:, :], psM[:, 0, :]).then_inc(s_xv, 1)
                elif kind == "max_turn":
                    dve.wait_ge(s_mt, b + 2)
                    if not (isinstance(b, int) and b < 0):
                        dve.wait_ge(s_mw, 16 * (b + 1))
                    dve.tensor_copy(mT[:, :], psMT[0:SPLITS * HEADS, :]).then_inc(s_mT, 1)
                elif kind == "v_proj":
                    dve.wait_ge(s_vp, b + 2)
                    v = v_s[1 - par][:, :, 0:9 * HEADS].rearrange("p c (h e) -> p c h e", e=9)[:, :, :, 0:HD]
                    dve.tensor_tensor(v, psM[:, 0, :].rearrange("p (c h e) -> p c h e", c=CH, e=HD),
                                      bv_s[:, None, :].to_broadcast([P, CH, D])
                                      .rearrange("p c (h e) -> p c h e", e=HD), ALU.add).then_inc(s_v, 1)
                elif kind in ("out0", "out1", "out2", "out3"):
                    c = int(kind[3])
                    src = (psV[:, :], psM[:, 1, :], psM[:, 0, :], psX[:, :])[c].rearrange("p (h e) -> p h e", e=32)
                    dve.wait_ge(s_outt, CH * b + c + 1)
                    dve.reciprocal(rden[:, c, :], src[:, :, HD]).then_inc(s_rd, 1)
                    dve.wait_ge(s_rd, CH * b + c + 1)
                    dve.tensor_tensor(att[:, c, :].rearrange("p (h e) -> p h e", e=HD), src[:, :, 0:HD],
                                      rden[:, c, :, None].to_broadcast([P, HEADS, HD]), ALU.mult).then_inc(s_norm, 1)
                elif kind == "wo":
                    dve.wait_ge(s_wo, b + 1)
                    dve.wait_ge(s_xb, b + 1)
                    if not (isinstance(b, int) and b >= MOE0):
                        scattered(b)
                    dve.tensor_tensor(xn[:, bass.ds(CH * b, CH), :], psM[:, 0, :].rearrange("p (c d) -> p c d", d=D),
                                      xres[:, :, :], ALU.add).then_inc(s_res, 1)
                elif kind == "slot_turn":
                    n = PER * (b - MOE0) + t
                    dve.wait_ge(s_xt, n + 1)
                    dve.tensor_copy(xT[t % 2][:, :], psS[:, 2, 0:SLOT]).then_inc(s_xT, 1)
                elif kind == "down":
                    n = PER * (b - MOE0) + t
                    dve.wait_ge(s_ym, n + 1)
                    dve.wait_ge(s_yst[t % 3], 16 * AHEAD + 16 * (PER // 3 * (b - MOE0) + t // 3))
                    w = w_e[t % 3][:, B3AT:B3AT + D]
                    dve.tensor_tensor(ys[t % 3][:, :, :], psS[:, 3, 0:2 * D].rearrange("p (c d) -> p c d", d=D),
                                      w[:, None, :].to_broadcast([P, 2, D]), ALU.add).then_inc(s_y, 1)

            def scattered(b):
                if is_moe[0]:
                    dve.wait_ge(s_scat, 2 * 16 * TILES)
                else:
                    dve.wait_ge(s_scat, 2 * 16 * 4 * CH * (b + 1))

            is_moe = [False]

            def route():
                logit, shifted, ex, w = wide[0:4]
                v3 = lambda a: a.rearrange("p (t e) -> p t e", e=NE)
                tok = lambda a: a[:, :, None].to_broadcast([P, TILES, NE])
                per_e = lambda a: a[:, None, :].to_broadcast([P, TILES, NE])
                col = [flat(ys[k // 4])[:, k % 4 * TILES:(k % 4 + 1) * TILES] for k in range(8)]
                dve.wait_ge(s_lread, 1)
                link(dve.tensor_reduce(col[0], v3(logit), AX.X, ALU.max))
                dve.tensor_tensor(v3(shifted), v3(logit), tok(col[0]), ALU.subtract).then_inc(s_gshift, 1)
                dve.wait_ge(s_gexp, 1)
                link(dve.tensor_reduce(col[1], v3(ex), AX.X, ALU.add))
                link(dve.reciprocal(col[2], col[1]))
                link(dve.tensor_tensor(v3(w), v3(ex), tok(col[2]), ALU.mult))
                picks = wide[4:6]
                for k, gate in enumerate((gate1, gate2)):
                    link(dve.tensor_reduce(gate[:, :], v3(w), AX.X, ALU.max))
                    link(dve.tensor_tensor(v3(wide[6]), v3(w), tok(gate[:, :]), ALU.is_equal))
                    link(dve.tensor_tensor(v3(wide[6]), v3(wide[6]), per_e(prio_s[:, :]), ALU.mult))
                    link(dve.tensor_reduce(col[3], v3(wide[6]), AX.X, ALU.max))
                    link(dve.tensor_tensor(v3(picks[k]), v3(wide[6]), tok(col[3]), ALU.is_equal))
                    if k == 0:
                        link(dve.scalar_tensor_tensor(out=w, in0=picks[0], scalar=-2.0, in1=w, op0=ALU.mult,
                                                      op1=ALU.add))
                dve.tensor_tensor(pair_b, picks[0], picks[1], ALU.add).then_inc(s_pick, 1)
                dve.wait_ge(s_rank, 1)
                in_tile, total = wide[0:2]
                dve.tensor_copy(in_tile, psM[:, 0, :])
                dve.tensor_copy(total, psM[:, 1, :])
                dve.tensor_copy(wide[2], psM[:, 1, :]).then_inc(s_ranked, 1)
                dve.wait_ge(s_ranked, 1)
                a, b_, n = wide[2], wide[3], 1
                while n < TILES:
                    dve.tensor_copy(b_[:, 0:n * NE], a[:, 0:n * NE])
                    link(dve.tensor_tensor(b_[:, n * NE:], a[:, n * NE:], a[:, :-n * NE], ALU.add))
                    a, b_, n = b_, a, 2 * n
                whole, ints = xT[0], xT[1][:, :].bitcast(I32)
                count = a[:, (TILES - 1) * NE:TILES * NE]
                link(dve.tensor_scalar(ints[:, 0:NE], count, float(SLOT - 1), None, ALU.add))
                link(dve.tensor_single_scalar(ints[:, NE:2 * NE], ints[:, 0:NE], SLOT.bit_length() - 1,
                                              ALU.logical_shift_right))
                link(dve.tensor_copy(whole[:, 0:NE], ints[:, NE:2 * NE]))
                dve.tensor_copy(whole[:, NE:2 * NE], whole[:, 0:NE])
                link(dve.tensor_tensor(wide[6], a, total, ALU.subtract))
                p, r, n = NE, 2 * NE, 1
                while n < NE:
                    dve.tensor_copy(whole[:, r:r + n], whole[:, p:p + n])
                    link(dve.tensor_tensor(whole[:, r + n:r + NE], whole[:, p + n:p + NE], whole[:, p:p + NE - n],
                                           ALU.add))
                    p, r, n = r, r + NE, 2 * n
                end, base = whole[:, p:p + NE], whole[:, r:r + NE]
                link(dve.tensor_tensor(base, end, whole[:, 0:NE], ALU.subtract))
                link(dve.tensor_scalar(base, base, float(SLOT), None, ALU.mult))
                link(dve.tensor_tensor(wide[6], wide[6], in_tile, ALU.add))
                link(dve.tensor_tensor(v3(wide[6]), v3(wide[6]), per_e(base), ALU.add))
                for k in range(2):
                    link(dve.tensor_tensor(wide[1], picks[k], wide[6], ALU.mult))
                    link(dve.tensor_reduce(col[4 + k], v3(wide[1]), AX.X, ALU.add))
                    link(dve.tensor_copy(slots[:, k, :], col[4 + k]))
                for t0 in range(0, ETILES, TILES):
                    t1 = min(ETILES, t0 + TILES)
                    c = wide[1][:, 0:(t1 - t0) * NE].rearrange("p (t e) -> p t e", e=NE)
                    link(dve.tensor_tensor(c, iota_s[:, t0:t1, None].to_broadcast([P, t1 - t0, NE]),
                                           end[:, None, :].to_broadcast([P, t1 - t0, NE]), ALU.is_ge))
                    link(dve.tensor_reduce(col[6][:, 0:t1 - t0], c, AX.X, ALU.add))
                    ins = dve.tensor_scalar(etile[:, t0:t1], col[6][:, 0:t1 - t0], float(NE - 1), None, ALU.min)
                    if t1 < ETILES:
                        link(ins)
                ins.then_inc(s_slots, 1)

            def combine(g):
                if g >= 2:
                    dve.wait_ge(s_out[g % 2], 16 * (g // 2))
                dve.wait_ge(s_gath[g % 2], 16 * 2 * CH * (g // 2 + 1))
                dve.wait_ge(s_res, AHEAD + g + 1)
                for k, gate in enumerate((gate1, gate2)):
                    for c in range(CH):
                        t = CH * g + c
                        before = xn[:, t, :] if k == 0 else outbuf[g % 2][:, c, :]
                        ins = dve.scalar_tensor_tensor(
                            out=outbuf[g % 2][:, c, :], in0=gathered[g % 2][:, CH * k + c, :],
                            scalar=gate[:, t:t + 1], in1=before, op0=ALU.mult, op1=ALU.add)
                    ins.then_inc((s_half, s_comb)[k], 1)
                    if k == 0:
                        dve.wait_ge(s_half, g + 1)

            layer_norm(0)
            dve.wait_ge(s_ones, 1)
            step("v_proj", None, -1, 1)
            layer_norm(1)
            for h in range(HEADS):
                max_unit(0, h)
            dve.wait_ge(s_logit, NB)
            dve.tensor_tensor(wide[0].rearrange("p (t e) -> p t e", e=NE), psV[:, :].rearrange("p (t e) -> p t e", e=NE),
                              gb_s[:, None, :].to_broadcast([P, TILES, NE]), ALU.add).then_inc(s_lread, 1)
            split_max(0)
            step("max_turn", None, -1, 1)
            dve.wait_ge(s_ones, 4)
            route()

            def body(b, i, par, moe):
                is_moe[0] = moe
                late = list(combined(b))
                for u in range(UNITS):
                    if has_next(b):
                        max_unit(b + 1, u)
                    if u % 3 == 0 and u and late:
                        combine(late.pop(0))
                if has_next(b):
                    split_max(b + 1)
                for kind, t in between(b, moe):
                    step(kind, t, b, par)

            batches(dve, body)
            combine(NB - 1)


def kernel(**inputs):
    import numpy as np
    import concourse.bacc as bacc
    from concourse.bass_utils import run_bass_kernel_spmd

    get = lambda n: np.asarray(inputs[n])
    x = np.ascontiguousarray(get("L0_attn_x"))
    rows = get("L0_attn_Wqkv").reshape(HEADS, 3, HD, D)
    bias = get("L0_attn_bqkv").reshape(HEADS, 3, HD)
    w1, w2, w3 = get("L0_ffn_w1"), get("L0_ffn_w2"), get("L0_ffn_w3")
    b1, b2, b3 = get("L0_ffn_b1"), get("L0_ffn_b2"), get("L0_ffn_b3")
    wall = np.concatenate([
        w1,
        w2.reshape(NE, 2, P, HID).transpose(0, 2, 1, 3).reshape(NE, P, 2 * HID),
        w3.reshape(NE, 2, P, D).transpose(0, 2, 1, 3).reshape(NE, P, 2 * D),
        np.broadcast_to(b3[:, None, :], (NE, P, D)),
        b1.reshape(NE, 2, P).transpose(0, 2, 1),
        b2.reshape(NE, 2, P).transpose(0, 2, 1)], axis=2)
    arrays = {
        "x": x,
        "wq": rows[:, 0].reshape(P, D).T, "wk": rows[:, 1].reshape(P, D).T, "wv": rows[:, 2].reshape(P, D).T,
        "wo": get("L0_attn_Wo").T,
        "bq": bias[:, 0].reshape(P, 1), "bk": bias[:, 1].reshape(P, 1), "bv": bias[:, 2].reshape(P),
        "bo": get("L0_attn_bo"), "gate_w": get("L0_ffn_gate_w"), "gate_b": get("L0_ffn_gate_b"), "wall": wall,
        "ident": np.eye(P, dtype=np.float32), "tri": np.triu(np.ones((P, P), np.float32), 1),
        "iota": np.arange(ETILES, dtype=np.float32), "prio": np.arange(NE, 0, -1).astype(np.float32),
    }
    arrays = {n: np.ascontiguousarray(a) for n, a in arrays.items()}
    nc = bacc.Bacc("TRN2", target_bir_lowering=False, num_devices=1)
    args = [nc.dram_tensor(f"in_{n}", a.shape, F32, kind="ExternalInput").ap() for n, a in arrays.items()]
    out = nc.dram_tensor("out", x.shape, F32, kind="ExternalOutput").ap()
    build_block_kernel(nc, *args, out)
    result = run_bass_kernel_spmd(nc, [{f"in_{n}": a for n, a in arrays.items()}], core_ids=[0])
    return result.results[0]["out"]
```

```python
import concourse.bass as bass
from concourse import mybir
from contextlib import ExitStack

F32, BF16, I32, U32 = mybir.dt.float32, mybir.dt.bfloat16, mybir.dt.int32, mybir.dt.uint32
ALU, ACT, AX = mybir.AluOpType, mybir.ActivationFunctionType, mybir.AxisListType
P = 128
HEADS, HD = 16, 8
NB, SEQ, D = 16, 512, 128
CH = SEQ // P
TILES = NB * CH
NE, HID = 8, 256
SPLITS = 3
STACK = SPLITS * SPLITS * HD
SROWS = STACK + SPLITS
QUAD = 4
UNITS = HEADS // QUAD * CH
VW = 9 * HEADS + 24
SLOT = 256
ETILES = 72
WCOLS = HID + 2 * HID + 2 * D + D + 4
W2AT, W3AT, B3AT, BIAT = HID, 3 * HID, 3 * HID + 2 * D, 3 * HID + 3 * D
MOE0, MOE1, PER = 4, 10, 12
WBUFS, XBUFS = 4, 3
assert PER % WBUFS == 0 and PER % XBUFS == 0
assert (MOE1 - MOE0) * PER == ETILES and ETILES * SLOT >= 2 * NB * SEQ + NE * (SLOT - 1)
EPS = 1e-5
SCALE = 1.0 / float(HD) ** 0.5


def build_block_kernel(nc, x, wq, wk, wv, wo, bq, bk, bv, bo, gate_w, gate_b, wall, ident, tri, iota, prio, out):
    with ExitStack() as ctx:
        def sb(name, shape, dt=F32):
            return ctx.enter_context(nc.sbuf_tensor(name, shape, dt))

        def sem(name):
            return ctx.enter_context(nc.semaphore(name))

        xn = sb("xn", [P, TILES, D])
        wq_s, wk_s, wv_s, wo_s = (sb(n, [P, P]) for n in ("wq_s", "wk_s", "wv_s", "wo_s"))
        bq_s, bk_s = sb("bq_s", [P, 1]), sb("bk_s", [P, 1])
        bv_s, bo_s = sb("bv_s", [P, D]), sb("bo_s", [P, D])
        gw_s, gb_s = sb("gw_s", [P, 32]), sb("gb_s", [P, NE])
        ident_s, ident_b = sb("ident_s", [P, P]), sb("ident_b", [P, P], BF16)
        prio_s, iota_s = sb("prio_s", [P, NE]), sb("iota_s", [P, ETILES])
        stats, small = sb("stats", [P, TILES, 6]), sb("small", [P, 6, TILES])
        gate1, gate2 = sb("gate1", [P, TILES]), sb("gate2", [P, TILES])
        slots = sb("slots", [P, 2, TILES], U32)
        etile = sb("etile", [P, ETILES], U32)
        xq_rows = sb("xq_rows", [P, CH, D])
        xqT, xvT = sb("xqT", [P, SEQ]), sb("xvT", [P, SEQ])
        qk_f, qk_r = sb("qk_f", [P, 2, SEQ]), sb("qk_r", [P, SEQ])
        parts = sb("parts", [P, 2, SPLITS, SEQ], BF16)
        qstack = [sb(f"qstack{i}", [P, HEADS, SEQ], BF16) for i in range(2)]
        kstack = [sb(f"kstack{i}", [P, HEADS, SEQ], BF16) for i in range(2)]
        v_s = [sb(f"v_s{i}", [P, CH, VW]) for i in range(2)]
        probs = sb("probs", [P, CH, QUAD, SEQ])
        mx, mr = sb("mx", [P, CH, HEADS]), sb("mr", [P, CH, HEADS])
        mparts = sb("mparts", [P, CH, SPLITS * HEADS], BF16)
        mT = sb("mT", [SPLITS * HEADS, SEQ], BF16)
        ot = sb("ot", [P, HEADS // QUAD, SEQ])
        rden, att = sb("rden", [P, CH, HEADS]), sb("att", [P, CH, D])
        attT, xres = sb("attT", [P, SEQ]), sb("xres", [P, CH, D])
        w_e = [sb(f"w_e{i}", [P, WCOLS]) for i in range(WBUFS)]
        xs = [sb(f"xs{i}", [P, 2, D]) for i in range(XBUFS)]
        ys = [sb(f"ys{i}", [P, 2, D]) for i in range(XBUFS)]
        xT = [sb(f"xT{i}", [P, SLOT]) for i in range(2)]
        h1, h2 = sb("h1", [P, 2, SLOT]), sb("h2", [P, 2, SLOT])
        ring = probs[:, :, :, :].rearrange("p a b c -> p (a b c)")

        def blocks(n, count):
            return ring[:, n * SEQ:(n + count) * SEQ]

        first_f = [qk_f] + [blocks(2 * g, 2).rearrange("p (s t) -> p s t", s=2) for g in range(2)]
        first_parts = [parts] + [blocks(4 + SPLITS * g, SPLITS).bitcast(BF16)
                                 .rearrange("p (s i t) -> p s i t", s=2, i=SPLITS) for g in range(2)]
        first_xT = [xqT, xvT, xqT]
        gate_xT = [blocks(10 + i, 1) for i in range(4)]
        gate_T = [blocks(14 + i, 1) for i in range(2)]
        flat = lambda a: a[:, :, :].rearrange("p c d -> p (c d)")
        wide = [w_e[i][:, k * SEQ:(k + 1) * SEQ] for i in range(3) for k in range(2)] + [flat(h2)]
        zeros = flat(h1)
        pair_b = flat(xs[0]).bitcast(BF16)
        tri_b, ones_b = flat(xs[1])[:, 0:64].bitcast(BF16), flat(xs[1])[:, 64:128].bitcast(BF16)
        tri_f = flat(xs[2])[:, 0:P]
        v3 = lambda a: a.rearrange("p (t e) -> p t e", e=NE)
        tok = lambda a: a[:, :, None].to_broadcast([P, TILES, NE])
        per_e = lambda a: a[:, None, :].to_broadcast([P, TILES, NE])
        col = [flat(ys[k // 4])[:, k % 4 * TILES:(k % 4 + 1) * TILES] for k in range(8)]
        logit, shifted, ex, w_gate = wide[0:4]
        picks, rank = wide[4:6], wide[6]
        counts, end, base = xT[0][:, 0:5 * NE], xT[1][:, 0:NE], xT[1][:, NE:2 * NE]
        gathered = [w_e[i][:, 0:2 * CH * D].rearrange("p (k d) -> p k d", d=D) for i in range(2)]
        outbuf = [w_e[2][:, i * CH * D:(i + 1) * CH * D].rearrange("p (c d) -> p c d", d=D) for i in range(2)]

        psS = ctx.enter_context(nc.psum_tensor("psS", [P, 4, 512], F32))
        psM = ctx.enter_context(nc.psum_tensor("psM", [P, 2, 512], F32))
        psV = ctx.enter_context(nc.psum_tensor("psV", [P, 512], F32))
        psX = ctx.enter_context(nc.psum_tensor("psX", [P, 512], F32))
        max_banks = [psM[:, 0, :], psM[:, 1, :], psX[:, :]]
        psMT = psX[:, 0:256].bitcast(BF16)

        stack_d = nc.dram_tensor("stack_rows", [2, 2, HEADS, STACK, SEQ], BF16, kind="Internal").ap()
        max_d = nc.dram_tensor("max_rows", [2, SPLITS * HEADS, SEQ], BF16, kind="Internal").ap()
        xt_d = nc.dram_tensor("turned_rows", [NB, P, SEQ], F32, kind="Internal").ap()
        xs_d = nc.dram_tensor("slot_rows", [ETILES * SLOT, D], F32, kind="Internal").ap()
        ys_d = nc.dram_tensor("slot_outs", [ETILES * SLOT, D], F32, kind="Internal").ap()
        xs_v = xs_d.rearrange("(n p c) d -> n p (c d)", p=P, c=2)
        ys_v = ys_d.rearrange("(n p c) d -> n p (c d)", p=P, c=2)
        x_v = x.rearrange("b (p c) d -> b p (c d)", c=CH)
        out_v = out.rearrange("b (p c) d -> b p (c d)", c=CH)

        LN_GROUPS = 4
        s_const, s_zero, s_cst, s_zset = sem("s_const"), sem("s_zero"), sem("s_cst"), sem("s_zset")
        s_gpad = sem("s_gpad")
        s_ones = sem("s_ones")
        ROWS = 16 * 2 * SPLITS
        CLEAR = 8 * P
        CONSTANTS = 16 * 14
        s_x = [sem(f"s_x{i}") for i in range(LN_GROUPS)]
        s_dve, s_pool = sem("s_dve"), sem("s_pool")
        s_var, s_sd = sem("s_var"), sem("s_sd")
        s_xn = sem("s_xn")
        s_gxt, s_gx, s_logit = sem("s_gxt"), sem("s_gx"), sem("s_logit")
        s_lt, s_ltt, s_lread = sem("s_lt"), sem("s_ltt"), sem("s_lread")
        s_gshift, s_gexp, s_gsum = sem("s_gshift"), sem("s_gexp"), sem("s_gsum")
        s_gdve, s_gpool = sem("s_gdve"), sem("s_gpool")
        s_etile = sem("s_etile")
        s_base = sem("s_base")
        s_pick, s_rank, s_ranked, s_slots = sem("s_pick"), sem("s_rank"), sem("s_ranked"), sem("s_slots")
        s_xqrow, s_xqt, s_xq = sem("s_xqrow"), sem("s_xqt"), sem("s_xq")
        s_keep, s_xvT = sem("s_keep"), sem("s_xvT")
        s_qp, s_kp, s_qf, s_kf = sem("s_qp"), sem("s_kp"), sem("s_qf"), sem("s_kf")
        s_part, s_rows = sem("s_part"), sem("s_rows")
        s_stack = [[sem(f"s_stack{i}{q}") for q in range(HEADS // QUAD)] for i in range(2)]
        s_vp, s_v = sem("s_vp"), sem("s_v")
        s_mxmm, s_mx, s_mp = sem("s_mxmm"), sem("s_mx"), sem("s_mp")
        s_mt, s_mT, s_mw, s_mrow = sem("s_mt"), sem("s_mT"), sem("s_mw"), sem("s_mrow")
        s_st, s_exp, s_pvu, s_ot = sem("s_st"), sem("s_exp"), sem("s_pvu"), sem("s_ot")
        s_outt, s_rd, s_norm = sem("s_outt"), sem("s_rd"), sem("s_norm")
        s_att, s_attT, s_wo = sem("s_att"), sem("s_attT"), sem("s_wo")
        s_xres, s_xb, s_res = sem("s_xres"), sem("s_xb"), sem("s_res")
        s_scat = sem("s_scat")
        s_w = [sem(f"s_w{i}") for i in range(WBUFS)]
        s_xs = [sem(f"s_xs{i}") for i in range(XBUFS)]
        s_yst = [sem(f"s_yst{i}") for i in range(XBUFS)]
        s_xt, s_xT, s_h1m, s_h1 = sem("s_xt"), sem("s_xT"), sem("s_h1m"), sem("s_h1")
        s_h2m, s_h2, s_ym, s_y = sem("s_h2m"), sem("s_h2"), sem("s_ym"), sem("s_y")
        s_gath = [sem(f"s_gath{i}") for i in range(2)]
        s_out = [sem(f"s_out{i}") for i in range(2)]
        AHEAD = 1
        s_half, s_comb = sem("s_half"), sem("s_comb")
        s_settled = sem("s_settled")

        GATES_FIRST = 11
        MAX_UNITS = 15

        AUX = ["max_turn", "pv_last", "xq_turn", "out0", "out1", "out2", "out3", "q_proj", "v_proj",
               "att_turn", "k_proj", "wo"]
        AUX_MOE = ["max_turn", "v_proj", "pv_last", "xq_turn", "q_proj", "k_proj",
                   "out0", "out1", "out2", "out3", "att_turn", "wo"]

        def between(b, moe):
            if not moe:
                return [(a, None) for a in AUX if (has_qk(b) or a not in ("xq_turn", "q_proj", "k_proj"))
                        and (has_next(b) or a not in ("max_turn", "v_proj"))]
            aux = [(a, None) for a in AUX_MOE]
            steps = aux[0:3] + [("slot_turn", 0), aux[3], ("slot_turn", 1), ("up", 0)] + aux[4:6]
            aux = aux[6:]
            for t in range(PER):
                steps.append(("mid", t))
                if t + 1 < PER:
                    steps.append(("up", t + 1))
                if t + 2 < PER:
                    steps.append(("slot_turn", t + 2))
                if t == 0 or len(aux) >= PER - t:
                    steps.append(aux.pop(0))
                steps.append(("down", t))
            return steps + aux

        def turned_out(c, moe):
            return (psV[:, :], psM[:, 1, :], psM[:, 0, :], psX[:, :])[c] if moe else psS[:, c, :]

        def settle(eng):
            eng.sem_inc(s_settled, 1)

        def has_qk(b):
            return not isinstance(b, int) or b + 3 < NB

        def has_next(b):
            return not isinstance(b, int) or b + 1 < NB

        COMBINED = {10: range(0, 3), 11: range(3, 6), 12: range(6, 8), 13: range(8, 10), 14: range(10, 12),
                    15: range(12, 15)}

        def combined(b):
            return COMBINED.get(b, range(0)) if isinstance(b, int) else range(0)

        def batches(eng, body, loop_first=True):
            if loop_first:
                with eng.Fori(0, MOE0 // 2) as i:
                    for par in range(2):
                        body(2 * i + par, i, par, False)
            else:
                for b in range(MOE0):
                    body(b, b // 2, b % 2, False)
            with eng.Fori(MOE0 // 2, MOE1 // 2) as i:
                for par in range(2):
                    body(2 * i + par, i, par, True)
            for b in range(MOE1, NB):
                body(b, b // 2, b % 2, False)

        block = ctx.enter_context(nc.Block())

        @block.sync
        def _(sp):
            for dst, src in ((xn[:, 0:2 * CH, :].rearrange("p (b c) d -> p b (c d)", c=CH), x_v[0:2]),
                             (xn[:, 2 * CH:4 * CH, :].rearrange("p (b c) d -> p b (c d)", c=CH), x_v[2:4])):
                sp.dma_start(dst, src.rearrange("b p k -> p b k")).then_inc(s_x[0], 16)
            for dst, src in ((ident_s[:, :], ident), (wq_s[:, :], wq), (wk_s[:, :], wk), (wv_s[:, :], wv),
                             (wo_s[:, :], wo), (bq_s[:, :], bq), (bk_s[:, :], bk),
                             (bv_s[:, :], bv.partition_broadcast(P)), (bo_s[:, :], bo.partition_broadcast(P)),
                             (gw_s[:, 0:NE], gate_w), (gb_s[:, :], gate_b.partition_broadcast(P)),
                             (prio_s[:, :], prio.partition_broadcast(P)), (iota_s[:, :], iota.partition_broadcast(P)),
                             (tri_f, tri)):
                sp.dma_start(dst, src).then_inc(s_const, 16)
            for b in range(4, NB, 2):
                sp.dma_start(xn[:, CH * b:CH * (b + 2), :].rearrange("p (b c) d -> p b (c d)", c=CH),
                             x_v[b:b + 2].rearrange("b p k -> p b k")).then_inc(s_x[b // 4], 16)

            def clear(first, last):
                for r in range(first * CLEAR, last * CLEAR, CLEAR):
                    sp.dma_start(xs_d[r:r + CLEAR, :].rearrange("(p r) d -> p (r d)", p=P)
                                 .rearrange("p (i k) -> p i k", i=2),
                                 zeros[:, None, :].to_broadcast([P, 2, SEQ])).then_inc(s_zero, 16)

            def write_rows(g, pair, par, parts=parts):
                sp.wait_ge(s_part, 8 * (g + 1))
                settle(sp)
                if not isinstance(g, int) or g >= 2:
                    for q in range(HEADS // QUAD):
                        sp.wait_ge(s_stack[par][q], 32 * pair)
                for i in range(SPLITS):
                    for side in range(2):
                        rows = stack_d[side, par].rearrange("h (d i j) t -> i j (h d) t", i=SPLITS, j=SPLITS)
                        for_part = rows[i] if side == 0 else rows[:, i]
                        sp.dma_start(for_part.rearrange("n p t -> p n t"),
                                     parts[:, side, i, None, :].to_broadcast([P, SPLITS, SEQ])) \
                            .then_inc(s_rows, 16)

            def keep_rows(g, src):
                sp.wait_ge(s_xq, g + 1)
                settle(sp)
                sp.dma_start(xt_d[bass.ds(g, 1)].rearrange("b p t -> (b p) t"), src[:, :]).then_inc(s_keep, 16)

            def read_rows(par, q):
                for side, stack in ((0, qstack), (1, kstack)):
                    sp.dma_start(stack[par][0:STACK, QUAD * q:QUAD * (q + 1), :],
                                 stack_d[side, par, QUAD * q:QUAD * (q + 1)].rearrange("h r t -> r h t")) \
                        .then_inc(s_stack[par][q], 16)

            def write_max(g, par):
                sp.wait_ge(s_mT, g + 1)
                sp.dma_start(max_d[par], mT[:, :]).then_inc(s_mw, 16)

            def read_max(g, par):
                sp.wait_ge(s_mw, 16 * (g + 1))
                sp.dma_start(qstack[par][STACK:SROWS, :, :],
                             max_d[par].rearrange("(s h) t -> s h t", s=SPLITS)).then_inc(s_mrow, 16)

            def expert_of(n):
                return sp.value_load(etile[0:1, bass.ds(n, 1)], min_val=0, max_val=NE - 1)

            def load_weights(e, t):
                sp.dma_start(w_e[t % WBUFS][:, :], wall[bass.ds(e, 1)].rearrange("e p n -> (e p) n")) \
                    .then_inc(s_w[t % WBUFS], 16)

            def load_rows(n, t):
                sp.dma_start(xs[t % XBUFS][:, :, :].rearrange("p c d -> p (c d)"),
                             xs_v[bass.ds(n, 1)].rearrange("n p k -> (n p) k")).then_inc(s_xs[t % XBUFS], 16)

            sp.wait_ge(s_zset, 1)
            clear(0, 6)
            for g in range(3):
                if g:
                    keep_rows(g, first_xT[g])
                write_rows(g, g // 2, g % 2, first_parts[g])
                if g < 2:
                    sp.wait_ge(s_rows, ROWS * (g + 1))
                    sp.wait_ge(s_ones, 2 * (g + 1))
                    for q in range(HEADS // QUAD):
                        read_rows(g, q)
                clear((6, 8, 10)[g], (8, 10, 18)[g])
            write_max(0, 0)
            read_max(0, 0)

            def body(b, i, par, moe):
                late = list(combined(b))
                if has_qk(b):
                    if not moe:
                        sp.wait_ge(s_xn, LN_GROUPS)
                    sp.wait_ge(s_xqt, b + 3)
                    sp.dma_start(xq_rows[:, :, :], xn[:, bass.ds(CH * (b + 3), CH), :]).then_inc(s_xqrow, 16)
                if has_next(b):
                    sp.wait_ge(s_vp, b + 1)
                    settle(sp)
                    sp.wait_ge(s_keep, 16 * (min(b + 2, NB - 1) if isinstance(b, int) else b + 2))
                    settle(sp)
                    sp.dma_start(xvT[:, :], xt_d[bass.ds(b + 1, 1)].rearrange("b p t -> (b p) t")).then_inc(s_xvT, 16)
                sp.wait_ge(s_res, AHEAD + b)
                sp.dma_start(xres[:, :, :].rearrange("p c d -> p (c d)"),
                             x_v[bass.ds(b, 1)].rearrange("b p k -> (b p) k")).then_inc(s_xres, 16)
                if moe:
                    sp.wait_ge(s_scat, 2 * 16 * TILES)
                    sp.wait_ge(s_etile, 1)
                    sp.wait_ge(s_y, AHEAD + PER * (b - MOE0))
                    settle(sp)
                    for t in range(WBUFS):
                        n = PER * (b - MOE0) + t
                        if t < XBUFS:
                            load_rows(n, t)
                        load_weights(expert_of(n), t)
                if not isinstance(b, int) or b + 2 < NB:
                    sp.wait_ge(s_rows, ROWS * (b + 3))
                    for q in range(HEADS // QUAD):
                        if q == HEADS // QUAD - 1 and has_next(b):
                            write_max(b + 1, 1 - par)
                            read_max(b + 1, 1 - par)
                        sp.wait_ge(s_st, 2 * UNITS * b + 2 * CH * (q + 1))
                        read_rows(par, q)
                        if q == 2 and late:
                            store_out(late.pop(0))
                elif has_next(b):
                    write_max(b + 1, 1 - par)
                    read_max(b + 1, 1 - par)
                for g in late:
                    store_out(g)
                if has_qk(b):
                    keep_rows(b + 3, xqT)
                for t in range(PER if moe else 0):
                    n = PER * (b - MOE0) + t
                    if t + XBUFS < PER:
                        sp.wait_ge(s_xt, n + 1)
                        load_rows(n + XBUFS, t)
                    if t + WBUFS < PER:
                        settle(sp)
                        e = expert_of(n + WBUFS)
                    sp.wait_ge(s_y, AHEAD + n + 1)
                    if t + WBUFS < PER:
                        load_weights(e, t)
                    sp.dma_start(ys_v[bass.ds(n, 1)].rearrange("n p k -> (n p) k"),
                                 ys[t % XBUFS][:, :, :].rearrange("p c d -> p (c d)")).then_inc(s_yst[t % XBUFS], 16)
                if has_qk(b):
                    write_rows(b + 3, i + (par + 3) // 2, 1 - par)

            def store_out(g):
                sp.wait_ge(s_comb, g + 1)
                sp.dma_start(out_v[g], outbuf[g % 2].rearrange("p c d -> p (c d)")).then_inc(s_out[g % 2], 16)

            batches(sp, body)
            store_out(NB - 1)
            for i in range(2):
                sp.wait_ge(s_out[i], 16 * NB // 2)

        @block.gpsimd
        def _(pool):
            def split(g, qk_f=qk_f, parts=parts, first=False):
                if not first:
                    pool.wait_ge(s_rows, ROWS * g)
                for side, s_f in ((0, s_qf), (1, s_kf)):
                    pool.wait_ge(s_f, g + 1)
                    settle(pool)
                    f, part = qk_f[:, side, :], [parts[:, side, i, :] for i in range(SPLITS)]
                    at = 8 * g + 4 * side
                    pool.tensor_scalar(part[0], f, 1.0, 0.0, ALU.mult, ALU.add).then_inc(s_part, 1)
                    pool.wait_ge(s_part, at + 1)
                    pool.tensor_tensor(qk_r[:, :], f, part[0], ALU.subtract).then_inc(s_part, 1)
                    pool.wait_ge(s_part, at + 2)
                    settle(pool)
                    pool.tensor_scalar(part[1], qk_r[:, :], 1.0, 0.0, ALU.mult, ALU.add).then_inc(s_part, 1)
                    pool.wait_ge(s_part, at + 3)
                    pool.tensor_tensor(part[2], qk_r[:, :], part[1], ALU.subtract).then_inc(s_part, 1)
                    pool.wait_ge(s_part, at + 4)

            done = [0]

            def link(ins):
                done[0] += 1
                ins.then_inc(s_pool, 1)
                pool.wait_ge(s_pool, done[0])

            def over_experts(dst, src, last=link):
                four = flat(ys[2])[:, 0:4 * TILES].rearrange("p (t e) -> p t e", e=4)
                two = flat(xs[2])[:, P:P + 2 * TILES].rearrange("p (t e) -> p t e", e=2)
                link(pool.tensor_tensor(four, src[:, :, 0:4], src[:, :, 4:8], ALU.add))
                link(pool.tensor_tensor(two, four[:, :, 0:2], four[:, :, 2:4], ALU.add))
                last(pool.tensor_tensor(dst[:, :, None], two[:, :, 0:1], two[:, :, 1:2], ALU.add))

            def route():
                w, tmp = w_gate, wide[1]
                pool.wait_ge(s_gdve, 1)
                pool.tensor_tensor(v3(shifted), v3(logit), tok(col[0]), ALU.subtract).then_inc(s_gshift, 1)
                pool.wait_ge(s_gexp, 1)
                over_experts(col[1], v3(ex), lambda ins: ins.then_inc(s_gsum, 1))
                pool.wait_ge(s_gdve, 2)
                pool.tensor_tensor(v3(w), v3(ex), tok(col[2]), ALU.mult).then_inc(s_gpool, 1)
                for k in range(2):
                    pool.wait_ge(s_gdve, 3 + 2 * k)
                    pool.tensor_tensor(v3(rank), v3(rank), per_e(prio_s[:, :]), ALU.mult).then_inc(s_gpool, 1)
                    pool.wait_ge(s_gdve, 4 + 2 * k)
                    if k == 0:
                        link(pool.tensor_tensor(w, w, picks[0], ALU.subtract))
                        pool.tensor_tensor(w, w, picks[0], ALU.subtract).then_inc(s_gpool, 1)
                pool.tensor_tensor(pair_b, picks[0], picks[1], ALU.add).then_inc(s_pick, 1)
                in_tile, total = wide[0:2]
                pool.wait_ge(s_ranked, 3)
                a, b_, n = wide[2], wide[3], 1
                while n < TILES:
                    link(pool.tensor_scalar(b_[:, 0:n * NE], a[:, 0:n * NE], 1.0, 0.0, ALU.mult, ALU.add))
                    link(pool.tensor_tensor(b_[:, n * NE:], a[:, n * NE:], a[:, :-n * NE], ALU.add))
                    a, b_, n = b_, a, 2 * n
                link(pool.tensor_tensor(rank, a, total, ALU.subtract))
                link(pool.tensor_tensor(rank, rank, in_tile, ALU.add))
                pool.wait_ge(s_base, 1)
                link(pool.tensor_tensor(v3(rank), v3(rank), per_e(base), ALU.add))
                for k in range(2):
                    link(pool.tensor_tensor(tmp, picks[k], rank, ALU.mult))
                    over_experts(col[4 + k], v3(tmp))
                    ins = pool.tensor_scalar(slots[:, k, :], col[4 + k], 1.0, 0.0, ALU.mult, ALU.add)
                    if k == 0:
                        link(ins)
                ins.then_inc(s_slots, 1)

            def scatter(g):
                for t in range(CH * g, CH * (g + 1)):
                    for k in range(2):
                        pool.indirect_dma_start(
                            out=xs_d, out_offset=bass.IndirectOffsetOnAxis(ap=slots[:, k, t:t + 1], axis=0),
                            in_=xn[:, t, :], in_offset=None).then_inc(s_scat, 16)

            def gather(g):
                if g >= 2:
                    pool.wait_ge(s_comb, g - 1)
                for k in range(2):
                    for c in range(CH):
                        t = CH * g + c
                        pool.indirect_dma_start(
                            out=gathered[g % 2][:, CH * k + c, :], out_offset=None, in_=ys_d,
                            in_offset=bass.IndirectOffsetOnAxis(ap=slots[:, k, t:t + 1], axis=0)) \
                            .then_inc(s_gath[g % 2], 16)

            pool.memset(zeros, 0.0).then_inc(s_zset, 1)
            pool.wait_ge(s_zset, 1)
            pool.memset(v_s[0][:, :, :], 1.0).then_inc(s_ones, 1)
            pool.wait_ge(s_ones, 1)
            pool.memset(kstack[0][64:96, :, :], 1.0).then_inc(s_ones, 1)
            pool.wait_ge(s_ones, 2)
            for g in range(3):
                split(g, first_f[g], first_parts[g], True)
                if g == 0:
                    pool.memset(kstack[1][64:96, :, :], 1.0).then_inc(s_ones, 1)
                    pool.wait_ge(s_ones, 3)
                    pool.memset(v_s[1][:, :, :], 1.0).then_inc(s_ones, 1)
                    pool.wait_ge(s_ones, 4)

            def body(b, i, par, moe):
                if isinstance(b, int) and b < MOE0:
                    if b == 0:
                        route()
                        pool.wait_ge(s_slots, 1)
                        pool.wait_ge(s_zero, 16 * ETILES * SLOT // CLEAR)
                        pool.wait_ge(s_xn, LN_GROUPS)
                    else:
                        pool.wait_ge(s_res, AHEAD + b)
                    for g in range(4 * b, 4 * b + 4):
                        scatter(g)
                for g in combined(b):
                    if g == 0:
                        for i in range(XBUFS):
                            pool.wait_ge(s_yst[i], 16 * AHEAD + 16 * ETILES // XBUFS)
                    gather(g)
                pool.wait_ge(s_xres, 16 * (b + 1))
                pool.tensor_tensor(xres[:, :, :], xres[:, :, :], bo_s[:, None, :].to_broadcast([P, CH, D]),
                                   ALU.add).then_inc(s_xb, 1)
                if has_qk(b):
                    split(b + 3)

            pool.wait_ge(s_const, CONSTANTS)
            batches(pool, body, loop_first=False)
            gather(NB - 1)

        @block.scalar
        def _(act):
            def deviation(i):
                act.wait_ge(s_var, i + 1)
                t0, t1 = TILES // LN_GROUPS * i, TILES // LN_GROUPS * (i + 1)
                act.activation(small[:, 3, t0:t1], small[:, 2, t0:t1], ACT.Sqrt).then_inc(s_sd, 1)

            def step(kind, t, b):
                if kind == "pv_last":
                    act.wait_ge(s_pvu, UNITS * (b + 1))
                    act.activation(ot[:, 3, :], psV[:, :], ACT.Copy).then_inc(s_ot, 1)
                elif kind == "xq_turn":
                    act.wait_ge(s_xqt, b + 4)
                    act.wait_ge(s_keep, 16 * (b + 2))
                    act.activation(xqT[:, :], psX[:, :], ACT.Copy).then_inc(s_xq, 1)
                elif kind == "q_proj":
                    act.wait_ge(s_qp, b + 4)
                    act.wait_ge(s_part, 8 * (b + 3))
                    act.activation(qk_f[:, 0, :], psM[:, 1, :], ACT.Identity, bias=bq_s[:, 0:1]).then_inc(s_qf, 1)
                elif kind == "k_proj":
                    act.wait_ge(s_kp, b + 4)
                    act.activation(qk_f[:, 1, :], psX[:, :], ACT.Identity, bias=bk_s[:, 0:1]).then_inc(s_kf, 1)
                elif kind == "att_turn":
                    act.wait_ge(s_att, b + 1)
                    act.activation(attT[:, :], psV[:, :], ACT.Copy).then_inc(s_attT, 1)
                elif kind in ("up", "mid"):
                    n = PER * (b - MOE0) + t
                    mm, done, bank, dst, at = (s_h1m, s_h1, 0, h1, BIAT) if kind == "up" else \
                        (s_h2m, s_h2, 1, h2, BIAT + 2)
                    act.wait_ge(mm, n + 1)
                    for c in range(2):
                        act.activation(dst[:, c, :], psS[:, bank, c * SLOT:(c + 1) * SLOT], ACT.Gelu,
                                       bias=w_e[t % WBUFS][:, at + c:at + c + 1]).then_inc(done, 1)

            act.wait_ge(s_const, CONSTANTS)
            def gate_out(i):
                act.wait_ge(s_logit, i + 1)
                if i >= 2:
                    act.wait_ge(s_ltt, i - 1)
                act.activation(gate_T[i % 2], psV[:, :], ACT.Copy).then_inc(s_lt, 1)

            deviation(0)
            for g in range(3):
                act.wait_ge(s_xqt, g + 1)
                if g == 2:
                    act.wait_ge(s_vp, 1)
                act.activation(first_xT[g][:, :], psS[:, g, :], ACT.Copy).then_inc(s_xq, 1)
                act.wait_ge(s_qp, g + 1)
                act.activation(first_f[g][:, 0, :], psM[:, 1, :], ACT.Identity, bias=bq_s[:, 0:1]).then_inc(s_qf, 1)
                act.wait_ge(s_kp, g + 1)
                act.activation(first_f[g][:, 1, :], psX[:, :], ACT.Identity, bias=bk_s[:, 0:1]).then_inc(s_kf, 1)
            for g in range(NB):
                if g % 4 == 0 and g // 4 + 1 < LN_GROUPS:
                    deviation(g // 4 + 1)
                act.wait_ge(s_gxt, g + 1)
                if g >= 4:
                    act.wait_ge(s_logit, g // 4)
                act.activation(gate_xT[g % 4], psS[:, g % 3, :], ACT.Copy).then_inc(s_gx, 1)
                if g % 4 == 0 and g:
                    gate_out(g // 4 - 1)
            gate_out(NB // 4 - 1)
            act.wait_ge(s_gshift, 1)
            act.activation(ex, shifted, ACT.Exp).then_inc(s_gexp, 1)
            act.wait_ge(s_rank, 1)
            for dst, i in ((wide[0], 0), (wide[1], 1), (wide[2], 1)):
                act.activation(dst, psM[:, i, :], ACT.Copy).then_inc(s_ranked, 1)
            act.wait_ge(s_ltt, NB // 4)
            act.wait_ge(s_rows, 3 * ROWS)

            def body(b, i, par, moe):
                for u in range(UNITS):
                    for half in range(2):
                        act.wait_ge(s_st, 2 * UNITS * b + 2 * u + half + 1)
                        if u >= CH and half == 0:
                            act.wait_ge(s_pvu, UNITS * b + u - CH + 1)
                        act.activation(probs[:, u % CH, 2 * half:2 * half + 2, :],
                                       psS[:, 2 * half:2 * half + 2, :], ACT.Exp, scale=SCALE).then_inc(s_exp, 1)
                    if u % CH == 0 and u:
                        q = u // CH - 1
                        act.wait_ge(s_pvu, UNITS * b + CH * (q + 1))
                        act.activation(ot[:, q, :], psV[:, :], ACT.Copy).then_inc(s_ot, 1)
                for kind, t in between(b, moe):
                    step(kind, t, b)

            batches(act, body)

        @block.tensor
        def _(pe):
            def turn_rows(dst, rows, done):
                for c in range(CH):
                    mm = pe.transpose(dst[:, c * P:(c + 1) * P], rows[:, c, :], ident_s[:, :])
                mm.then_inc(done, 1)

            def max_tiles(g, pair, par, first, last):
                for i in range(first, last):
                    h, c = i // CH, i % CH
                    if i % (QUAD * CH) == 0:
                        pe.wait_ge(s_stack[par][h // QUAD], 32 * (pair + 1))
                    if i >= 3:
                        pe.wait_ge(s_mx, 4 * HEADS * g + i - 2)
                    pe.matmul(max_banks[i % 3], qstack[par][0:STACK, h, c * P:(c + 1) * P],
                              kstack[par][0:STACK, h, :], start=True, stop=True).then_inc(s_mxmm, 1)

            def pv_unit(b, par, u):
                q, kc = u // CH, u % CH
                pe.wait_ge(s_exp, 2 * UNITS * b + 2 * u + 2)
                if kc == 0 and q:
                    pe.wait_ge(s_ot, 4 * b + q)
                if u == 0:
                    pe.wait_ge(s_res, AHEAD + b)
                for j in range(QUAD):
                    h = QUAD * q + j
                    mm = pe.matmul(psV[32 * j:32 * (j + 1), :], v_s[par][:, kc, 9 * h:9 * h + 32],
                                   probs[:, u % CH, j, :], start=(kc == 0), stop=(kc == CH - 1),
                                   tile_position=(0, 32 * j))
                mm.then_inc(s_pvu, 1)
                return mm

            def step(kind, t, b, par, moe=False):
                if kind == "pv_last":
                    pv_unit(b, par, UNITS - 1)
                elif kind == "xq_turn":
                    pe.wait_ge(s_xqrow, 16 * (b + 1))
                    pe.wait_ge(s_mT, b + 2)
                    turn_rows(psX, xq_rows, s_xqt)
                elif kind == "max_turn":
                    pe.wait_ge(s_mp, 4 * (b + 2))
                    settle(pe)
                    for c in range(CH):
                        mm = pe.transpose(psMT[0:SPLITS * HEADS, c * P:(c + 1) * P], mparts[:, c, :], ident_b[:, :])
                    mm.then_inc(s_mt, 1)
                elif kind == "q_proj":
                    pe.wait_ge(s_xq, b + 4)
                    pe.wait_ge(s_mx, 4 * HEADS * (b + 2))
                    pe.matmul(psM[:, 1, :], wq_s[:, :], xqT[:, :], start=True, stop=True).then_inc(s_qp, 1)
                elif kind == "k_proj":
                    pe.matmul(psX[:, :], wk_s[:, :], xqT[:, :], start=True, stop=True).then_inc(s_kp, 1)
                elif kind == "v_proj":
                    pe.wait_ge(s_xvT, 16 * (b + 1))
                    pe.wait_ge(s_mx, 4 * HEADS * (b + 2))
                    for c in range(CH):
                        mm = pe.matmul(psM[:, 0, c * P:(c + 1) * P], xvT[:, c * P:(c + 1) * P], wv_s[:, :],
                                       start=True, stop=True)
                    mm.then_inc(s_vp, 1)
                elif kind in ("out0", "out1", "out2", "out3"):
                    c = int(kind[3])
                    if c == 0:
                        pe.wait_ge(s_ot, 4 * b + 4)
                    elif moe:
                        pe.wait_ge((s_qf, s_v, s_kf)[c - 1], b + (4, 2, 4)[c - 1])
                    dst = turned_out(c, moe)
                    for q in range(HEADS // QUAD):
                        mm = pe.transpose(dst[:, q * P:(q + 1) * P], ot[:, q, c * P:(c + 1) * P], ident_s[:, :])
                    mm.then_inc(s_outt, 1)
                elif kind == "att_turn":
                    pe.wait_ge(s_norm, CH * (b + 1))
                    turn_rows(psV[:, :], att, s_att)
                elif kind == "wo":
                    pe.wait_ge(s_attT, b + 1)
                    for c in range(CH):
                        mm = pe.matmul(psV[:, c * P:(c + 1) * P], attT[:, c * P:(c + 1) * P], wo_s[:, :],
                                       start=True, stop=True)
                    mm.then_inc(s_wo, 1)
                else:
                    n, w = PER * (b - MOE0) + t, w_e[t % WBUFS]
                    landed = 16 * (PER // XBUFS * (b - MOE0) + t // XBUFS + 1)
                    if kind == "slot_turn":
                        pe.wait_ge(s_xs[t % XBUFS], landed)
                        if t:
                            pe.wait_ge(s_xT, n)
                        for c in range(2):
                            mm = pe.transpose(psS[:, 2, c * P:(c + 1) * P], xs[t % XBUFS][:, c, :], ident_s[:, :])
                        mm.then_inc(s_xt, 1)
                    elif kind == "up":
                        pe.wait_ge(s_w[t % WBUFS], 16 * (PER // WBUFS * (b - MOE0) + t // WBUFS + 1))
                        pe.wait_ge(s_xT, n + 1)
                        if t:
                            pe.wait_ge(s_h1, 2 * n)
                        for c in range(2):
                            mm = pe.matmul(psS[:, 0, c * SLOT:(c + 1) * SLOT], w[:, c * P:(c + 1) * P],
                                           xT[t % 2][:, :], start=True, stop=True)
                        mm.then_inc(s_h1m, 1)
                    elif kind == "mid":
                        pe.wait_ge(s_h1, 2 * n + 2)
                        if t:
                            pe.wait_ge(s_h2, 2 * n)
                        for c in range(2):
                            for k in range(2):
                                at = W2AT + k * HID + c * P
                                mm = pe.matmul(psS[:, 1, c * SLOT:(c + 1) * SLOT], w[:, at:at + P], h1[:, k, :],
                                               start=(k == 0), stop=(k == 1))
                        mm.then_inc(s_h2m, 1)
                    elif kind == "down":
                        pe.wait_ge(s_h2, 2 * n + 2)
                        if t:
                            pe.wait_ge(s_y, AHEAD + n)
                        for c in range(2):
                            for k in range(2):
                                at = W3AT + k * D
                                mm = pe.matmul(psS[:, 3, c * P:(c + 1) * P], h2[:, k, c * P:(c + 1) * P],
                                               w[:, at:at + D], start=(k == 0), stop=(k == 1))
                        mm.then_inc(s_ym, 1)

            pe.wait_ge(s_const, CONSTANTS)
            pe.wait_ge(s_gpad, 1)
            pe.wait_ge(s_xn, 1)
            for g in range(3):
                turn_rows(psS[:, g, :], xn[:, CH * g:CH * (g + 1), :], s_xqt)
            for g in range(3):
                pe.wait_ge(s_xq, g + 1)
                if g:
                    pe.wait_ge(s_qf, g)
                pe.matmul(psM[:, 1, :], wq_s[:, :], first_xT[g][:, :], start=True, stop=True).then_inc(s_qp, 1)
                if g:
                    pe.wait_ge(s_kf, g)
                pe.matmul(psX[:, :], wk_s[:, :], first_xT[g][:, :], start=True, stop=True).then_inc(s_kp, 1)
                if g == 0:
                    for c in range(CH):
                        mm = pe.matmul(psM[:, 0, c * P:(c + 1) * P], xqT[:, c * P:(c + 1) * P], wv_s[:, :],
                                       start=True, stop=True)
                    mm.then_inc(s_vp, 1)

            def gate(g):
                if g < NB:
                    if g % 4 == 0:
                        pe.wait_ge(s_xn, g // 4 + 1)
                    if g >= 3:
                        pe.wait_ge(s_gx, g - 2)
                    turn_rows(psS[:, g % 3, :], xn[:, CH * g:CH * (g + 1), :], s_gxt)
                if 0 < g <= NB and g % 4 == 0:
                    pe.wait_ge(s_gx, g)
                    if g > 4:
                        pe.wait_ge(s_lt, g // 4 - 1)
                    for j in range(4):
                        mm = pe.matmul(psV[32 * j:32 * (j + 1), :], gw_s[:, :], gate_xT[j], start=True, stop=True,
                                       tile_position=(0, 32 * j))
                    mm.then_inc(s_logit, 1)
                if 4 < g <= NB + 1 and g % 4 == 1:
                    four = g // 4 - 1
                    pe.wait_ge(s_lt, four + 1)
                    if four:
                        pe.wait_ge(s_lread, four)
                    for c in range(CH):
                        mm = pe.transpose(psS[:, 3, c * P:(c + 1) * P], gate_T[four % 2][:, c * P:(c + 1) * P],
                                          ident_s[:, :])
                    mm.then_inc(s_ltt, 1)

            pe.wait_ge(s_v, 1)
            pe.wait_ge(s_qf, 3)
            pe.wait_ge(s_kf, 3)
            for g in range(GATES_FIRST):
                gate(g)
            for h in range(HEADS):
                gate(GATES_FIRST + h)
                max_tiles(0, 0, 0, CH * h, CH * (h + 1))
            pe.wait_ge(s_lread, NB // 4)
            pe.wait_ge(s_cst, 1)
            step("max_turn", None, -1, 1)
            pe.wait_ge(s_pick, 1)
            pe.wait_ge(s_mx, 4 * HEADS)
            for i, m in enumerate((tri_b, ones_b)):
                mm = pe.matmul(psM[:, i, :], m, pair_b, start=True, stop=True)
            mm.then_inc(s_rank, 1)
            pe.wait_ge(s_ranked, 3)
            pe.wait_ge(s_mT, 1)

            def body(b, i, par, moe):
                pe.wait_ge(s_mrow, 16 * (b + 1))
                tiles = [min(4 * HEADS, 4 * HEADS * u // MAX_UNITS) for u in range(UNITS + 1)]
                for u in range(UNITS):
                    q, kc = u // CH, u % CH
                    cuts = [min(tiles[u] + n, tiles[u + 1]) for n in range(3)] + [tiles[u + 1]]
                    for half in range(2):
                        if u == 0 and half == 1:
                            if moe:
                                pe.wait_ge(s_y, AHEAD + PER * (b - MOE0))
                            elif isinstance(b, int):
                                pe.wait_ge(s_y, AHEAD + ETILES)
                        if u:
                            pe.wait_ge(s_exp, 2 * UNITS * b + 2 * u + half - 1)
                        for j in range(2 * half, 2 * half + 2):
                            h = QUAD * q + j
                            mm = pe.matmul(psS[:, j, :], kstack[par][0:SROWS, h, kc * P:(kc + 1) * P],
                                           qstack[par][0:SROWS, h, :], start=True, stop=True)
                        mm.then_inc(s_st, 1)
                        if u == 0 and half == 0:
                            pe.wait_ge(s_v, b + 1)
                            pe.wait_ge(s_qf, min(b + 3, NB) if isinstance(b, int) else b + 3)
                            pe.wait_ge(s_kf, min(b + 3, NB) if isinstance(b, int) else b + 3)
                        if has_next(b):
                            max_tiles(b + 1, i + (par + 1) // 2, 1 - par, cuts[half], cuts[half + 1])
                    if u:
                        pv_unit(b, par, u - 1)
                    if has_next(b):
                        max_tiles(b + 1, i + (par + 1) // 2, 1 - par, cuts[2], cuts[3])
                for kind, t in between(b, moe):
                    step(kind, t, b, par, moe)

            batches(pe, body)

        @block.vector
        def _(dve):
            done = [0]

            def link(ins):
                done[0] += 1
                ins.then_inc(s_dve, 1)
                dve.wait_ge(s_dve, done[0])

            dve.sem_inc(s_res, AHEAD)
            dve.sem_inc(s_y, AHEAD)
            for place in s_yst:
                dve.sem_inc(place, 16 * AHEAD)
            def statistics(i):
                t0, t1 = TILES // LN_GROUPS * i, TILES // LN_GROUPS * (i + 1)
                dve.wait_ge(s_x[i], 16 * 2)
                for t in range(t0, t1):
                    ins = dve.bn_stats(stats[:, t, :], xn[:, t, :])
                link(ins)
                st = stats[:, t0:t1, :]
                mean, tmp, var, sq = (small[:, k, t0:t1] for k in (0, 1, 2, 5))
                dve.tensor_tensor(sq, st[:, :, 1], st[:, :, 4], ALU.subtract)
                dve.tensor_tensor(tmp, st[:, :, 2], st[:, :, 5], ALU.add)
                link(dve.tensor_tensor(mean, st[:, :, 1], st[:, :, 4], ALU.add))
                dve.tensor_scalar(mean, mean, 0.5, None, ALU.mult)
                link(dve.tensor_tensor(sq, sq, sq, ALU.mult))
                link(dve.tensor_scalar(sq, sq, 0.25, EPS, ALU.mult, ALU.add))
                dve.scalar_tensor_tensor(out=var, in0=tmp, scalar=1.0 / D, in1=sq, op0=ALU.mult,
                                         op1=ALU.add).then_inc(s_var, 1)

            def normalise(i):
                t0, t1 = TILES // LN_GROUPS * i, TILES // LN_GROUPS * (i + 1)
                dve.wait_ge(s_sd, i + 1)
                link(dve.reciprocal(small[:, 4, t0:t1], small[:, 3, t0:t1]))
                for t in range(t0, t1):
                    ins = dve.tensor_scalar(xn[:, t, :], xn[:, t, :], small[:, 0, t:t + 1], small[:, 4, t:t + 1],
                                            ALU.subtract, ALU.mult)
                ins.then_inc(s_xn, 1)

            def max_unit(g, h):
                for c in range(CH):
                    dve.wait_ge(s_mxmm, 4 * HEADS * g + CH * h + c + 1)
                    dve.reduce_max(mx[:, c, h:h + 1], max_banks[(CH * h + c) % 3], AX.X).then_inc(s_mx, 1)

            def split_max(g):
                part = [mparts[:, :, HEADS * i:HEADS * (i + 1)] for i in range(SPLITS)]
                dve.wait_ge(s_mx, 4 * HEADS * (g + 1))
                dve.tensor_scalar(part[0], mx[:, :, :], -1.0, None, ALU.mult).then_inc(s_mp, 1)
                dve.wait_ge(s_mp, 4 * g + 1)
                dve.scalar_tensor_tensor(out=mr[:, :, :], in0=mx[:, :, :], scalar=-1.0, in1=part[0], op0=ALU.mult,
                                         op1=ALU.subtract).then_inc(s_mp, 1)
                dve.wait_ge(s_mp, 4 * g + 2)
                dve.tensor_copy(part[1], mr[:, :, :]).then_inc(s_mp, 1)
                dve.wait_ge(s_mp, 4 * g + 3)
                dve.tensor_tensor(part[2], mr[:, :, :], part[1], ALU.subtract).then_inc(s_mp, 1)

            def step(kind, t, b, par, moe=False):
                if kind == "max_turn":
                    dve.wait_ge(s_mt, b + 2)
                    if not (isinstance(b, int) and b < 0):
                        dve.wait_ge(s_mw, 16 * (b + 1))
                    dve.tensor_copy(mT[:, :], psMT[0:SPLITS * HEADS, :]).then_inc(s_mT, 1)
                elif kind == "v_proj":
                    dve.wait_ge(s_vp, b + 2)
                    v = v_s[1 - par][:, :, 0:9 * HEADS].rearrange("p c (h e) -> p c h e", e=9)[:, :, :, 0:HD]
                    dve.tensor_tensor(v, psM[:, 0, :].rearrange("p (c h e) -> p c h e", c=CH, e=HD),
                                      bv_s[:, None, :].to_broadcast([P, CH, D])
                                      .rearrange("p c (h e) -> p c h e", e=HD), ALU.add).then_inc(s_v, 1)
                elif kind in ("out0", "out1", "out2", "out3"):
                    c = int(kind[3])
                    src = turned_out(c, moe).rearrange("p (h e) -> p h e", e=32)
                    dve.wait_ge(s_outt, CH * b + c + 1)
                    dve.reciprocal(rden[:, c, :], src[:, :, HD]).then_inc(s_rd, 1)
                    dve.wait_ge(s_rd, CH * b + c + 1)
                    dve.tensor_tensor(att[:, c, :].rearrange("p (h e) -> p h e", e=HD), src[:, :, 0:HD],
                                      rden[:, c, :, None].to_broadcast([P, HEADS, HD]), ALU.mult).then_inc(s_norm, 1)
                elif kind == "wo":
                    dve.wait_ge(s_wo, b + 1)
                    dve.wait_ge(s_xb, b + 1)
                    if not (isinstance(b, int) and b >= MOE0):
                        scattered(b)
                    dve.tensor_tensor(xn[:, bass.ds(CH * b, CH), :], psV[:, :].rearrange("p (c d) -> p c d", d=D),
                                      xres[:, :, :], ALU.add).then_inc(s_res, 1)
                elif kind == "slot_turn":
                    n = PER * (b - MOE0) + t
                    dve.wait_ge(s_xt, n + 1)
                    dve.tensor_copy(xT[t % 2][:, :], psS[:, 2, 0:SLOT]).then_inc(s_xT, 1)
                elif kind == "down":
                    n = PER * (b - MOE0) + t
                    dve.wait_ge(s_ym, n + 1)
                    dve.wait_ge(s_yst[t % XBUFS], 16 * AHEAD + 16 * (PER // XBUFS * (b - MOE0) + t // XBUFS))
                    w = w_e[t % WBUFS][:, B3AT:B3AT + D]
                    dve.tensor_tensor(ys[t % XBUFS][:, :, :], psS[:, 3, 0:2 * D].rearrange("p (c d) -> p c d", d=D),
                                      w[:, None, :].to_broadcast([P, 2, D]), ALU.add).then_inc(s_y, 1)

            def scattered(b):
                if is_moe[0]:
                    dve.wait_ge(s_scat, 2 * 16 * TILES)
                else:
                    dve.wait_ge(s_scat, 2 * 16 * 4 * CH * (b + 1))

            is_moe = [False]

            def read_logits(i):
                dve.wait_ge(s_ltt, i + 1)
                for j in range(4):
                    dst = logit[:, NE * CH * (4 * i + j):NE * CH * (4 * i + j + 1)].rearrange("p (c e) -> p c e", e=NE)
                    src = psS[:, 3, :].rearrange("p (c j e) -> p j c e", c=CH, j=4)[:, j, :, 0:NE]
                    ins = dve.tensor_tensor(dst, src, gb_s[:, None, :].to_broadcast([P, CH, NE]), ALU.add)
                ins.then_inc(s_lread, 1)

            ROUTED = (6, 8, 9, 10, 11, 13)

            def route(n):
                if n == 0:
                    dve.wait_ge(s_lread, NB // 4)
                    dve.tensor_reduce(col[0], v3(logit), AX.X, ALU.max).then_inc(s_gdve, 1)
                elif n == 1:
                    dve.wait_ge(s_gsum, 1)
                    dve.reciprocal(col[2], col[1]).then_inc(s_gdve, 1)
                else:
                    k = n // 2 - 1
                    gate = (gate1, gate2)[k]
                    dve.wait_ge(s_gpool, n - 1)
                    if n % 2 == 0:
                        link(dve.tensor_reduce(gate[:, :], v3(w_gate), AX.X, ALU.max))
                        dve.tensor_tensor(v3(rank), v3(w_gate), tok(gate[:, :]), ALU.is_equal).then_inc(s_gdve, 1)
                    else:
                        link(dve.tensor_reduce(col[3], v3(rank), AX.X, ALU.max))
                        dve.tensor_tensor(v3(picks[k]), v3(rank), tok(col[3]), ALU.is_equal).then_inc(s_gdve, 1)

            def place_experts():
                dve.wait_ge(s_ranked, 2)
                ints = counts[:, 4 * NE:5 * NE].bitcast(I32)
                count = counts[:, 0:NE]
                link(dve.tensor_reduce(count, wide[1].rearrange("p (t e) -> p e t", e=NE), AX.X, ALU.add))
                link(dve.tensor_scalar(ints, count, float(SLOT - 1), None, ALU.add))
                link(dve.tensor_single_scalar(ints, ints, SLOT.bit_length() - 1, ALU.logical_shift_right))
                link(dve.tensor_copy(counts[:, 0:NE], ints))
                link(dve.tensor_copy(counts[:, NE:2 * NE], ints))
                p, r, n = NE, 2 * NE, 1
                while n < NE:
                    dve.tensor_copy(counts[:, r:r + n], counts[:, p:p + n])
                    link(dve.tensor_tensor(counts[:, r + n:r + NE], counts[:, p + n:p + NE], counts[:, p:p + NE - n],
                                           ALU.add))
                    p, r, n = r, (r % (3 * NE)) + NE, 2 * n
                link(dve.tensor_copy(end, counts[:, p:p + NE]))
                link(dve.tensor_tensor(base, end, counts[:, 0:NE], ALU.subtract))
                dve.tensor_scalar(base, base, float(SLOT), None, ALU.mult).then_inc(s_base, 1)
                c = stats[:, :, :].rearrange("p t k -> p (t k)")
                for t0 in range(0, ETILES, ETILES // 2):
                    n = ETILES // 2
                    marks = v3(c[:, 0:n * NE])
                    link(dve.tensor_tensor(marks, iota_s[:, t0:t0 + n, None].to_broadcast([P, n, NE]),
                                           end[:, None, :].to_broadcast([P, n, NE]), ALU.is_ge))
                    link(dve.tensor_reduce(c[:, n * NE:n * NE + n], marks, AX.X, ALU.add))
                    ins = dve.tensor_scalar(etile[:, t0:t0 + n], c[:, n * NE:n * NE + n], float(NE - 1), None, ALU.min)
                    if t0 == 0:
                        link(ins)
                ins.then_inc(s_etile, 1)

            def combine(g, first=0, last=2 * CH):
                if first == 0:
                    if g >= 2:
                        dve.wait_ge(s_out[g % 2], 16 * (g // 2))
                    dve.wait_ge(s_gath[g % 2], 16 * 2 * CH * (g // 2 + 1))
                    dve.wait_ge(s_res, AHEAD + g + 1)
                for n in range(first, last):
                    k, c = n // CH, n % CH
                    t = CH * g + c
                    if n == CH:
                        dve.wait_ge(s_half, g + 1)
                    before = xn[:, t, :] if k == 0 else outbuf[g % 2][:, c, :]
                    ins = dve.scalar_tensor_tensor(
                        out=outbuf[g % 2][:, c, :], in0=gathered[g % 2][:, CH * k + c, :],
                        scalar=(gate1, gate2)[k][:, t:t + 1], in1=before, op0=ALU.mult, op1=ALU.add)
                    if n == CH - 1:
                        ins.then_inc(s_half, 1)
                    if n == 2 * CH - 1:
                        ins.then_inc(s_comb, 1)

            dve.memset(gw_s[:, NE:32], 0.0).then_inc(s_gpad, 1)
            statistics(0)
            normalise(0)
            dve.wait_ge(s_const, CONSTANTS)
            dve.tensor_copy(ident_b[:, :], ident_s[:, :])
            dve.tensor_copy(tri_b, tri_f)
            dve.memset(ones_b, 1.0).then_inc(s_cst, 1)
            dve.wait_ge(s_ones, 1)
            step("v_proj", None, -1, 1)
            statistics(1)
            for i in range(1, LN_GROUPS):
                if i + 1 < LN_GROUPS:
                    statistics(i + 1)
                normalise(i)
            for i in range(NB // 4):
                if 4 * i + 5 < GATES_FIRST:
                    read_logits(i)
            for h in range(HEADS):
                max_unit(0, h)
                if (h + GATES_FIRST) % 4 == 1 and h + GATES_FIRST <= NB + 1:
                    read_logits((h + GATES_FIRST) // 4 - 1)
                if h in ROUTED:
                    route(ROUTED.index(h))
            split_max(0)
            step("max_turn", None, -1, 1)
            place_experts()
            dve.wait_ge(s_ones, 4)

            def body(b, i, par, moe):
                is_moe[0] = moe
                late = list(combined(b))
                for u in range(UNITS):
                    if has_next(b):
                        max_unit(b + 1, u)
                    n = 2 * ((u - 5) % 5)
                    if late and 5 <= u < UNITS - 1 and n < 2 * CH:
                        combine(late[0], n, n + 2)
                        if n + 2 == 2 * CH:
                            late.pop(0)
                if has_next(b):
                    split_max(b + 1)
                for kind, t in between(b, moe):
                    step(kind, t, b, par, moe)
                    if late and kind == ("v_proj" if has_next(b) else "out3"):
                        combine(late.pop(0))

            batches(dve, body)
            combine(NB - 1)


def kernel(**inputs):
    import numpy as np
    import concourse.bacc as bacc
    from concourse.bass_utils import run_bass_kernel_spmd

    get = lambda n: np.asarray(inputs[n])
    x = np.ascontiguousarray(get("L0_attn_x"))
    rows = get("L0_attn_Wqkv").reshape(HEADS, 3, HD, D)
    bias = get("L0_attn_bqkv").reshape(HEADS, 3, HD)
    w1, w2, w3 = get("L0_ffn_w1"), get("L0_ffn_w2"), get("L0_ffn_w3")
    b1, b2, b3 = get("L0_ffn_b1"), get("L0_ffn_b2"), get("L0_ffn_b3")
    wall = np.concatenate([
        w1,
        w2.reshape(NE, 2, P, HID).transpose(0, 2, 1, 3).reshape(NE, P, 2 * HID),
        w3.reshape(NE, 2, P, D).transpose(0, 2, 1, 3).reshape(NE, P, 2 * D),
        np.broadcast_to(b3[:, None, :], (NE, P, D)),
        b1.reshape(NE, 2, P).transpose(0, 2, 1),
        b2.reshape(NE, 2, P).transpose(0, 2, 1)], axis=2)
    arrays = {
        "x": x,
        "wq": rows[:, 0].reshape(P, D).T, "wk": rows[:, 1].reshape(P, D).T, "wv": rows[:, 2].reshape(P, D).T,
        "wo": get("L0_attn_Wo").T,
        "bq": bias[:, 0].reshape(P, 1), "bk": bias[:, 1].reshape(P, 1), "bv": bias[:, 2].reshape(P),
        "bo": get("L0_attn_bo"), "gate_w": get("L0_ffn_gate_w"), "gate_b": get("L0_ffn_gate_b"), "wall": wall,
        "ident": np.eye(P, dtype=np.float32), "tri": np.triu(np.ones((P, P), np.float32), 1),
        "iota": np.arange(ETILES, dtype=np.float32), "prio": np.arange(NE, 0, -1).astype(np.float32),
    }
    arrays = {n: np.ascontiguousarray(a) for n, a in arrays.items()}
    nc = bacc.Bacc("TRN2", target_bir_lowering=False, num_devices=1)
    args = [nc.dram_tensor(f"in_{n}", a.shape, F32, kind="ExternalInput").ap() for n, a in arrays.items()]
    out = nc.dram_tensor("out", x.shape, F32, kind="ExternalOutput").ap()
    build_block_kernel(nc, *args, out)
    result = run_bass_kernel_spmd(nc, [{f"in_{n}": a for n, a in arrays.items()}], core_ids=[0])
    return result.results[0]["out"]
```
